# Optimizing a Trainium2 kernel written in Bass

```python
import numpy as np
import jax
import jax.numpy as jnp

def _softmax(x, axis=-1):
    return jax.nn.softmax(x, axis=axis)

def _gelu(x):
    return jax.nn.gelu(x, approximate=True)

def _silu(x):
    return jax.nn.silu(x)

def _sigmoid(x):
    return jax.nn.sigmoid(x)

def _layernorm(x, axis=-1, eps=1e-05):
    m = jnp.mean(x, axis=axis, keepdims=True)
    v = jnp.var(x, axis=axis, keepdims=True)
    return (x - m) / jnp.sqrt(v + eps)

def _scatter_add(tgt, idx, src, axis=0):
    return tgt.at[idx].add(src)

def _segment_sum(src, seg, n):
    return jax.ops.segment_sum(src, seg, n)
kernel_name = 'mk_decoder_preln_d1_seqx_r4_eece21'

def setup_inputs(seed: int=0):
    np.random.seed(seed)
    _w = jnp.asarray

    def _rec_inputs():
        import jax
        import jax.numpy as jnp
        _rk = jax.random.key(seed)
        x = -0.0002928 + 1 * jax.random.normal(jax.random.fold_in(_rk, 1), (32, 128, 256), jnp.float32)
        _lenS = 128 - jax.random.randint(jax.random.fold_in(_rk, 7), (32,), 0, max(1, 128 // 4) + 1, jnp.int32)
        _lenS2 = 128 - jax.random.randint(jax.random.fold_in(_rk, 8), (32,), 0, max(1, 128 // 4) + 1, jnp.int32)
        _ctx_1024P = jax.random.normal(jax.random.fold_in(_rk, 11), (32, 16, 256), jnp.float32)
        _ctx_1024c = jax.random.dirichlet(jax.random.fold_in(_rk, 511), 0.3 * jnp.ones((16,), jnp.float32), (32, 128))
        _ctx_1024t = jnp.einsum('bsk,bkd->bsd', _ctx_1024c, _ctx_1024P)
        _ctx_1024t = _ctx_1024t * jax.lax.rsqrt(jnp.mean(jnp.square(_ctx_1024t)) + 1e-12) * 0.953939
        ctx_1024 = -1.39393e-06 + 0.999914 * (_ctx_1024t + 0.3 * jax.random.normal(jax.random.fold_in(_rk, 611), (32, 128, 256), jnp.float32))
        return (x, ctx_1024)
    x, ctx_1024 = _rec_inputs()

    def _L0_attn_setup():
        import jax, jax.numpy as jnp
        import numpy as np
        HEADS = 16
        HIDDEN = 256
        key = jax.random.key(seed)
        ks = jax.random.split(key, 9)
        E, H = (256, HIDDEN)
        N, L = (4, 512)
        s = 0.02
        return {'X_embed': jax.random.normal(ks[0], (N, L, E), dtype=jnp.float32), 'Wq': jax.random.normal(ks[1], (E, H), dtype=jnp.float32) * s, 'bq': jax.random.normal(ks[2], (H,), dtype=jnp.float32) * s, 'Wk': jax.random.normal(ks[3], (E, H), dtype=jnp.float32) * s, 'bk': jax.random.normal(ks[4], (H,), dtype=jnp.float32) * s, 'Wv': jax.random.normal(ks[5], (E, H), dtype=jnp.float32) * s, 'bv': jax.random.normal(ks[6], (H,), dtype=jnp.float32) * s, 'Wo': jax.random.normal(ks[7], (H, H), dtype=jnp.float32) * s, 'bo': jax.random.normal(ks[8], (H,), dtype=jnp.float32) * s}
    _L0_attn_all = _L0_attn_setup()
    _L0_attn_in = {k: v for k, v in _L0_attn_all.items() if k in ('Wq', 'bq', 'Wk', 'bk', 'Wv', 'bv', 'Wo', 'bo')}
    del _L0_attn_all

    def _L0_xattn_setup():
        import jax, jax.numpy as jnp
        import numpy as np
        D_MODEL = 256
        NUM_HEADS = 16
        D_HEAD = D_MODEL // NUM_HEADS
        WINDOW = 128

        def _to_heads(x):
            B, S, _ = x.shape
            return x.reshape(B, S, NUM_HEADS, D_HEAD).transpose(0, 2, 1, 3)
        key = jax.random.key(seed)
        ks = jax.random.split(key, 12)
        B, S, D = (2, 512, D_MODEL)
        scale = 1.0 / np.sqrt(D)
        inp = {'query': jax.random.normal(ks[0], (B, S, D), jnp.float32), 'key': jax.random.normal(ks[1], (B, S, D), jnp.float32), 'value': jax.random.normal(ks[2], (B, S, D), jnp.float32), 'Wq': jax.random.normal(ks[3], (D, D), jnp.float32) * scale, 'bq': jnp.zeros((D,), jnp.float32), 'Wk': jax.random.normal(ks[4], (D, D), jnp.float32) * scale, 'bk': jnp.zeros((D,), jnp.float32), 'Wv': jax.random.normal(ks[5], (D, D), jnp.float32) * scale, 'bv': jnp.zeros((D,), jnp.float32), 'Wo': jax.random.normal(ks[6], (D, D), jnp.float32) * scale, 'bo': jnp.zeros((D,), jnp.float32)}
        return inp
    _L0_xattn_all = _L0_xattn_setup()
    _L0_xattn_in = {k: v for k, v in _L0_xattn_all.items() if k in ('Wq', 'bq', 'Wk', 'bk', 'Wv', 'bv', 'Wo', 'bo')}
    del _L0_xattn_all

    def _L0_ffn_setup():
        import jax, jax.numpy as jnp
        import numpy as np
        K_TOP = 2
        key = jax.random.key(seed)
        k1, k2, k3 = jax.random.split(key, 3)
        B, S, H, E = (4, 512, 256, 8)
        hidden_states = jax.random.normal(k1, (B, S, H), dtype=jnp.float32)
        router_w = jax.random.normal(k2, (E, H), dtype=jnp.float32) * 0.02
        expert_weights = jax.random.normal(k3, (E, H, H), dtype=jnp.float32) * 0.02
        return {'hidden_states': hidden_states, 'router_w': router_w, 'expert_weights': expert_weights}
    _L0_ffn_all = _L0_ffn_setup()
    _L0_ffn_in = {k: v for k, v in _L0_ffn_all.items() if k in ('router_w', 'expert_weights')}
    del _L0_ffn_all
    return {'x': x, 'ctx_1024': ctx_1024, 'L0_attn_Wq': _L0_attn_in['Wq'], 'L0_attn_bq': _L0_attn_in['bq'], 'L0_attn_Wk': _L0_attn_in['Wk'], 'L0_attn_bk': _L0_attn_in['bk'], 'L0_attn_Wv': _L0_attn_in['Wv'], 'L0_attn_bv': _L0_attn_in['bv'], 'L0_attn_Wo': _L0_attn_in['Wo'], 'L0_attn_bo': _L0_attn_in['bo'], 'L0_xattn_Wq': _L0_xattn_in['Wq'], 'L0_xattn_bq': _L0_xattn_in['bq'], 'L0_xattn_Wk': _L0_xattn_in['Wk'], 'L0_xattn_bk': _L0_xattn_in['bk'], 'L0_xattn_Wv': _L0_xattn_in['Wv'], 'L0_xattn_bv': _L0_xattn_in['bv'], 'L0_xattn_Wo': _L0_xattn_in['Wo'], 'L0_xattn_bo': _L0_xattn_in['bo'], 'L0_ffn_router_w': _L0_ffn_in['router_w'], 'L0_ffn_expert_weights': _L0_ffn_in['expert_weights']}

def reference(x, ctx_1024, L0_attn_Wq, L0_attn_bq, L0_attn_Wk, L0_attn_bk, L0_attn_Wv, L0_attn_bv, L0_attn_Wo, L0_attn_bo, L0_xattn_Wq, L0_xattn_bq, L0_xattn_Wk, L0_xattn_bk, L0_xattn_Wv, L0_xattn_bv, L0_xattn_Wo, L0_xattn_bo, L0_ffn_router_w, L0_ffn_expert_weights):
    import jax
    import jax.numpy as jnp

    def _L0_attn_ref(X_embed, Wq, bq, Wk, bk, Wv, bv, Wo, bo):
        import jax, jax.numpy as jnp
        import numpy as np
        HEADS = 16
        HIDDEN = 256
        N, L, _ = X_embed.shape
        H, heads = (HIDDEN, HEADS)
        dh = H // heads
        Q = X_embed @ Wq + bq
        K = X_embed @ Wk + bk
        V = X_embed @ Wv + bv
        Q = Q.reshape(N, heads, L, dh)
        K = K.reshape(N, heads, L, dh)
        V = V.reshape(N, heads, L, dh)
        scale = np.float32(1.0 / np.sqrt(H))
        Q = Q * scale
        K = K * scale
        scores = jnp.einsum('neax,nebx->neab', Q, K)
        A = jax.nn.softmax(scores, axis=2)
        Out = jnp.einsum('neab,neax->neax', A, V)
        Out = Out.reshape(N, L, H)
        return Out @ Wo + bo

    def _L0_xattn_ref(query, key, value, Wq, bq, Wk, bk, Wv, bv, Wo, bo):
        import jax, jax.numpy as jnp
        import numpy as np
        D_MODEL = 256
        NUM_HEADS = 16
        D_HEAD = D_MODEL // NUM_HEADS
        WINDOW = 128

        def _to_heads(x):
            B, S, _ = x.shape
            return x.reshape(B, S, NUM_HEADS, D_HEAD).transpose(0, 2, 1, 3)
        B, S, D = query.shape
        q = _to_heads(query @ Wq + bq)
        k = _to_heads(key @ Wk + bk)
        v = _to_heads(value @ Wv + bv)
        scores = jnp.einsum('bhqd,bhkd->bhqk', q, k) / jnp.sqrt(jnp.float32(D_HEAD))
        i = jnp.arange(S)[:, None]
        j = jnp.arange(S)[None, :]
        local_mask = jnp.abs(i - j) <= WINDOW // 2
        scores = jnp.where(local_mask[None, None], scores, -jnp.inf)
        attn = jax.nn.softmax(scores, axis=-1)
        ctx = jnp.einsum('bhqk,bhkd->bhqd', attn, v)
        ctx = ctx.transpose(0, 2, 1, 3).reshape(B, S, D)
        return ctx @ Wo + bo

    def _L0_ffn_ref(hidden_states, router_w, expert_weights):
        import jax, jax.numpy as jnp
        import numpy as np
        K_TOP = 2
        B, S, H = hidden_states.shape
        x = hidden_states.reshape(-1, H)
        logits = x @ router_w.T
        probs = jax.nn.softmax(logits, axis=-1)
        topk_vals, topk_idx = jax.lax.top_k(probs, K_TOP)
        topk_w = topk_vals / (topk_vals.sum(-1, keepdims=True) + 1e-06)
        expert_out = jnp.einsum('nh,eho->eno', x, expert_weights)
        combined = jnp.take_along_axis(expert_out.transpose(1, 0, 2), topk_idx[:, :, None], axis=1)
        combined = combined.transpose(1, 0, 2)
        remap_bias = jnp.take_along_axis(probs, topk_idx, axis=1).T[:, :, None]
        weights = topk_w.T[:, :, None]
        out = ((combined + remap_bias) * weights).sum(axis=0)
        return out.reshape(B, S, H)
    x = x + _L0_attn_ref(_layernorm(x, axis=-1), L0_attn_Wq, L0_attn_bq, L0_attn_Wk, L0_attn_bk, L0_attn_Wv, L0_attn_bv, L0_attn_Wo, L0_attn_bo)
    x = x + _L0_xattn_ref(_layernorm(x, axis=-1), ctx_1024, ctx_1024, L0_xattn_Wq, L0_xattn_bq, L0_xattn_Wk, L0_xattn_bk, L0_xattn_Wv, L0_xattn_bv, L0_xattn_Wo, L0_xattn_bo)
    x = x + _L0_ffn_ref(_layernorm(x, axis=-1), L0_ffn_router_w, L0_ffn_expert_weights)
    return x

_drawn_inputs = setup_inputs


def setup_inputs(seed=0):
    import zlib

    import numpy as np

    out = dict(_drawn_inputs(seed))
    spreads = {'L0_xattn_bq': (0.0, 0.1),
     'L0_xattn_bk': (0.0, 2.0),
     'L0_xattn_bv': (0.0, 0.1),
     'L0_xattn_bo': (0.0, 0.1)}
    factors = {'L0_attn_Wq': 64.0,
     'L0_attn_bq': 64.0,
     'L0_attn_Wk': 64.0,
     'L0_attn_bk': 192.458,
     'L0_attn_bv': 3.926}
    for name, (base, spread) in spreads.items():
        noise = np.random.default_rng([zlib.crc32(name.encode()), seed]).standard_normal(out[name].shape)
        drawn = base * np.exp(spread * noise) if base else spread * noise
        out[name] = jnp.asarray(drawn.astype(out[name].dtype))
    for name, factor in factors.items():
        out[name] = (out[name] * factor).astype(out[name].dtype)
    return out
```

```python
from contextlib import ExitStack

import concourse.bass as bass
from concourse import mybir

F32 = mybir.dt.float32
F32R = mybir.dt.float32r
BF16 = mybir.dt.bfloat16
ACT = mybir.ActivationFunctionType
ALU = mybir.AluOpType
AX = mybir.AxisListType

P = 128
EPS = 1e-5
TOP_EPS = 1e-6
WINDOW = 128
MASKED = -1e30
PAIR = 2

PROJECT, SELF, CROSS, EXPERTS = range(4)
STAGES = 4

BANK_USERS = [
    ("turn_o2", EXPERTS, True), ("turn_ctx", CROSS, True), ("out2", EXPERTS, False),
    ("k2", CROSS, True), ("v2", CROSS, False), ("turn_h3", EXPERTS, True),
    ("turn_w", SELF, False), ("turn_h1", PROJECT, True), ("q1", PROJECT, True),
    ("k1", PROJECT, True), ("turn_o1", SELF, True), ("v1", PROJECT, False),
    ("out1", SELF, False), ("turn_h2", SELF, True), ("q2", SELF, True),
]
BANKS = 3


def decoder_layer(nc, x, ctx, wq1, bq1, wk1, bk1, wv1, bv1, wo1, bo1,
                  wq2, bq2, wk2, bk2, wv2, bv2, wo2, bo2, router, experts, out):
    BATCHES, TOK, D = x.shape
    EX = router.shape[0]
    HEADS = 16
    HD = D // HEADS
    C = D // P
    G = P // HD
    NG = BATCHES // PAIR
    ROWS = 3 * HD
    UNITS = HEADS // 2
    FUNITS = PAIR * EX // 2
    TOK2 = PAIR * TOK
    SCALE1 = float(D) ** -0.5
    SCALE2 = float(HD) ** -0.5
    assert TOK == P and D == C * P and BATCHES % PAIR == 0 and 2 * ROWS <= P and UNITS % 4 == 0
    FIRST, LAST = STAGES, NG

    def active(i, stage):
        return not isinstance(i, int) or 0 <= i - stage < NG

    def order(i, name, rounded=False):
        users = [(n, s) for n, s, r in BANK_USERS if r or not rounded]
        at = [n for n, _ in users].index(name)
        if isinstance(i, int):
            return (sum(active(k, s) for k in range(i) for _, s in users)
                    + sum(active(i, s) for _, s in users[:at]))
        return order(FIRST, users[0][0], rounded) + len(users) * (i - FIRST) + at

    def bank_of(name):
        return [n for n, _, _ in BANK_USERS].index(name) % BANKS

    def emptied_before(i, name):
        if not isinstance(i, int):
            return order(i, name) - BANKS + 1
        at = [n for n, _, _ in BANK_USERS].index(name)
        before = [(k, p) for k in range(i + 1) for p, (_, s, _) in enumerate(BANK_USERS)
                  if (k, p) < (i, at) and p % BANKS == at % BANKS and active(k, s)]
        return order(before[-1][0], BANK_USERS[before[-1][1]][0]) + 1 if before else 0

    def wait(eng, sem, value):
        if not isinstance(value, int) or value > 0:
            eng.wait_ge(sem, value)

    def wait_alone(eng, sem, value):
        if not isinstance(value, int) or value > 0:
            eng.wait_ge(sem, value)
            eng.sem_inc(passed[eng.engine], 1)

    stack = ExitStack()
    with stack:
        def sb(name, shape, dt=F32):
            return stack.enter_context(nc.sbuf_tensor(name, shape, dt))

        def ps(name, shape):
            return stack.enter_context(nc.psum_tensor(name, shape, F32))

        def sem(name):
            return stack.enter_context(nc.semaphore(name))

        names = ["q1", "k1", "v1", "o1", "q2", "k2", "v2", "o2"]
        w_dram = dict(zip(names, [wq1, wk1, wv1, wo1, wq2, wk2, wv2, wo2]))
        w_scale = {n: {"q1": SCALE1, "k1": SCALE1, "q2": SCALE2}.get(n, 1.0) for n in names}
        W = {n: sb(f"w_{n}", [P, 2, C, D], F32R) for n in names}
        WE = sb("w_experts", [P, 2, C, EX * D], F32R)
        router_raw = sb("router_raw", [EX, D])
        router_t = sb("router_t", [P, C, EX])
        b_dram = {"q1": bq1, "k1": bk1, "q2": bq2, "k2": bk2}
        bcol_raw = sb("bcol_raw", [P, 4, C])
        bcol = sb("bcol", [P, 4, C])
        B_AT = {n: k for k, n in enumerate(b_dram)}
        brow = sb("brow", [P, 4, D])
        R_AT = {"v1": 0, "o1": 1, "v2": 2, "o2": 3}
        ident = sb("ident", [P, P])
        ident_bf = sb("ident_bf", [P, P], BF16)
        mask_bf = sb("mask_bf", [P, P], BF16)
        minus_half = sb("minus_half", [P, PAIR])
        falling = sb("falling", [P, PAIR, EX])

        x_in = sb("x_in", [P, PAIR, D])
        c_in = sb("c_in", [P, PAIR, D])
        x_o1 = sb("x_o1", [P, PAIR, D])
        x1 = sb("x1", [P, PAIR, D])
        x1_o2 = sb("x1_o2", [P, PAIR, D])
        x2 = sb("x2", [P, PAIR, D])
        h = [sb(f"h{k + 1}", [P, PAIR, D]) for k in range(3)]
        stats = [sb(f"stats{k + 1}", [P, PAIR, 6]) for k in range(3)]
        moments = [sb(f"moments{k + 1}", [P, PAIR, 2]) for k in range(3)]
        rstd = [sb(f"rstd{k + 1}", [P, PAIR]) for k in range(3)]
        v1 = sb("v1", [P, PAIR, D])
        v2 = sb("v2", [P, PAIR, D])
        o1 = sb("o1", [P, PAIR, D])
        o2 = sb("o2", [P, PAIR, D])
        turned_o = sb("turned_o", [P, 2, C, TOK2], F32R)
        turned_in = sb("turned_in", [P, 2, C, TOK2], F32R)
        turned_h = sb("turned_h", [P, 2, C, TOK2], F32R)
        q_split = sb("q_split", [P, 2, C, TOK2], F32R)
        k_split = sb("k_split", [P, 2, C, TOK2], F32R)
        ks1_in = sb("ks1_in", [PAIR * ROWS, HEADS, TOK], F32R)
        ks1 = sb("ks1", [PAIR * ROWS, HEADS, TOK], F32R)
        qs1 = sb("qs1", [PAIR * ROWS, PAIR, HEADS, TOK], F32R)
        qs2 = sb("qs2", [PAIR * ROWS, HEADS, TOK], F32R)
        ks2 = sb("ks2", [PAIR * ROWS, PAIR, HEADS, TOK], F32R)
        nmax1 = sb("nmax1", [P, UNITS, 4])
        nmax2 = sb("nmax2", [P, UNITS, 4])
        sum1 = sb("sum1", [P, PAIR, HEADS])
        sum2 = sb("sum2", [P, PAIR, HEADS])
        rsum1 = sb("rsum1", [P, PAIR, HEADS])
        rsum2 = sb("rsum2", [P, PAIR, HEADS])
        w_col = sb("w_col", [P, PAIR * HEADS])
        w_row = sb("w_row", [PAIR * HEADS, 8, HEADS])
        w_tok = sb("w_tok", [P, PAIR, HEADS])
        r_nmax = sb("r_nmax", [P, PAIR])
        r_exp = sb("r_exp", [P, PAIR, EX])
        r_sum = sb("r_sum", [P, PAIR])
        r_rsum = sb("r_rsum", [P, PAIR])
        r_p = sb("r_p", [P, PAIR, EX])
        r_rest = sb("r_rest", [P, PAIR, EX])
        r_eq = sb("r_eq", [P, PAIR, EX])
        r_key = sb("r_key", [P, PAIR, EX])
        r_first = sb("r_first", [P, PAIR])
        r_hot = [sb(f"r_hot{j}", [P, PAIR, EX]) for j in range(2)]
        r_top = sb("r_top", [P, PAIR, 2])
        r_norm = sb("r_norm", [P, PAIR])
        r_rnorm = sb("r_rnorm", [P, PAIR])
        r_w = sb("r_w", [P, PAIR, 2])
        r_pw = sb("r_pw", [P, PAIR, 2])
        r_wh = [sb(f"r_wh{j}", [P, PAIR, EX]) for j in range(2)]
        r_c = sb("r_c", [P, PAIR, EX])
        r_bias = sb("r_bias", [P, PAIR])
        space = sb("space", [P, 8192])
        w_raw = {n: space[:, 512 * k:512 * k + 512].rearrange("p (c n) -> p c n", c=C)
                 for k, n in enumerate(names)}
        e_raw = space[:, 4096:8192].rearrange("p (c n) -> p c n", c=C)
        SLOTS = 4
        e1 = space[:, 0:2048].rearrange("p (s h b a) -> p s h b a", s=SLOTS, h=2, b=PAIR)
        e2 = space[:, 2048:4096].rearrange("p (s h b a) -> p s h b a", s=SLOTS, h=2, b=PAIR)
        e2_t = space[:, 4096:5120].rearrange("p (s h b a) -> p s h b a", s=2, h=2, b=PAIR)
        scaled = space[:, 5120:6144].rearrange("p (s n) -> p s n", s=4)
        y = space[:, 6144:6656].rearrange("p (b n) -> p b n", b=PAIR)

        scores = ps("scores", [P, 2, 512])
        bank = ps("bank", [P, BANKS, 512])
        turned_e = ps("turned_e", [P, 512])
        attended = ps("attended", [P, 512])
        small = ps("small", [P, 512])
        w_sum = small[:, 0:PAIR * HEADS]
        logits = attended[:, 0:PAIR * EX].rearrange("p (b e) -> p b e", b=PAIR)
        router_ps = small[:, 128:128 + C * EX].rearrange("p (c e) -> p c e", c=C)

        relay = {n: nc.dram_tensor(f"relay_{n}", [2, D, PAIR, TOK], F32, kind="Internal").ap()
                 for n in ("q1", "k1", "q2", "k2")}

        weights_in, experts_in, bias_in, router_in = sem("weights_in"), sem("experts_in"), sem("bias_in"), sem("router_in")
        ident_zero, ident_ready, zeros_ready = sem("ident_zero"), sem("ident_ready"), sem("zeros_ready")
        mask_ready, falling_ready = sem("mask_ready"), sem("falling_ready")
        w_high, w_low, bcol_ready = sem("w_high"), sem("w_low"), sem("bcol_ready")
        router_turned, router_ready = sem("router_turned"), sem("router_ready")
        x_loaded, c_loaded, stored = sem("x_loaded"), sem("c_loaded"), sem("stored")
        bank_filled, bank_rounded, bank_emptied = sem("bank_filled"), sem("bank_rounded"), sem("bank_emptied")
        ln_stats = [sem(f"ln_stats{k + 1}") for k in range(3)]
        ln_moments = [sem(f"ln_moments{k + 1}") for k in range(3)]
        ln_rstd = [sem(f"ln_rstd{k + 1}") for k in range(3)]
        ln_done = [sem(f"ln_done{k + 1}") for k in range(3)]
        relay_in = {n: sem(f"relay_in_{n}") for n in relay}
        relay_out = {n: sem(f"relay_out_{n}") for n in relay}
        self_scored, self_maxed, self_exped = sem("self_scored"), sem("self_maxed"), sem("self_exped")
        self_inverted, self_weighed = sem("self_inverted"), sem("self_weighed")
        w_copied, w_spread, o1_ready = sem("w_copied"), sem("w_spread"), sem("o1_ready")
        w_row_ready, k1_laid = sem("w_row_ready"), sem("k1_laid")
        x_o1_ready, x1_ready, x1_o2_ready, x2_ready = sem("x_o1_ready"), sem("x1_ready"), sem("x1_o2_ready"), sem("x2_ready")
        cross_scored, cross_maxed, cross_exped = sem("cross_scored"), sem("cross_maxed"), sem("cross_exped")
        cross_turned, e2_by_act, e2_by_dve = sem("cross_turned"), sem("e2_by_act"), sem("e2_by_dve")
        cross_attended, cross_inverted, o2_ready = sem("cross_attended"), sem("cross_inverted"), sem("o2_ready")
        logits_ready, r_maxed, r_exped = sem("logits_ready"), sem("r_maxed"), sem("r_exped")
        r_step, routed = sem("r_step"), sem("routed")
        expert_ready, base_ready, first_summed, second_scaled, second_summed = (
            sem("expert_ready"), sem("base_ready"), sem("first_summed"), sem("second_scaled"), sem("second_summed"))

        passed = {e: sem(f"passed_{n}") for n, e in (("sp", nc.sync.engine), ("pool", nc.gpsimd.engine), ("dve", nc.vector.engine))}

        block = stack.enter_context(nc.Block())

        x_g = x.rearrange("(g b) t c -> g t b c", b=PAIR)
        c_g = ctx.rearrange("(g b) t c -> g t b c", b=PAIR)
        out_g = out.rearrange("(g b) t c -> g t b c", b=PAIR)

        def pipeline(eng, iteration):
            for i in range(FIRST):
                iteration(i)
            with eng.Fori(FIRST, LAST) as i:
                iteration(i)
            for i in range(LAST, NG + STAGES - 1):
                iteration(i)

        @block.sync
        def _(sp):
            with nc.allow_non_contiguous_dma("biases by channel, once"):
                sp.dma_start(x_in[:], x_g[0]).then_inc(x_loaded, 16)
                for n in names:
                    sp.dma_start(w_raw[n], w_dram[n].rearrange("(c p) n -> p c n", p=P)).then_inc(weights_in, 16)
                for n, b in b_dram.items():
                    sp.dma_start(bcol_raw[:, B_AT[n], :], b.rearrange("(c p) -> p c", p=P)).then_inc(bias_in, 16)
                for n, b in (("v1", bv1), ("o1", bo1), ("v2", bv2), ("o2", bo2)):
                    sp.dma_start(brow[:, R_AT[n], :], b.partition_broadcast(P)).then_inc(bias_in, 16)
                sp.dma_start(router_raw[:], router).then_inc(router_in, 16)

            for c in range(C):
                sp.dma_start(e_raw[:, c, :].rearrange("p (e n) -> p e n", n=D),
                             experts[:, c * P:(c + 1) * P, :].rearrange("e p n -> p e n")).then_inc(experts_in, 16)
            sp.wait_ge(zeros_ready, 2)

            def relay_write(g, n, split, done):
                wait_alone(sp, bank_emptied, done)
                wait_alone(sp, relay_out[n], 6 * 16 * g)
                sp.dma_start(relay[n].rearrange("s (c p) b t -> p s c (b t)", p=P),
                             split[:].bitcast(F32)).then_inc(relay_in[n], 16)

            def relay_read(g, n, target, parts, scored, count=UNITS):
                wait_alone(sp, relay_in[n], 16 * (g + 1))
                wait_alone(sp, scored, count * g)
                for b in range(PAIR):
                    for j, part in enumerate(parts):
                        row = b * ROWS + j * HD
                        to = target[row:row + HD, b] if len(target.shape) == 4 else target[row:row + HD]
                        sp.dma_start(to.bitcast(F32),
                                     relay[n][part, :, b, :].rearrange("(g x) t -> x g t", x=HD))\
                            .then_inc(relay_out[n], 16)

            def iteration(i):
                if active(i, CROSS):
                    g = i - CROSS
                    relay_read(g, "q2", qs2, (0, 0, 1), cross_scored)
                    relay_write(g, "k2", k_split, order(i, "k2") + 1)
                    relay_read(g, "k2", ks2, (0, 1, 0), cross_scored)
                if active(i, SELF):
                    if active(i, CROSS):
                        wait_alone(sp, bank_filled, order(i, "turn_ctx") + 1)
                    sp.dma_start(c_in[:], c_g[i - SELF]).then_inc(c_loaded, 16)
                if active(i, SELF):
                    g = i - SELF
                    wait_alone(sp, w_row_ready, g + 1)
                    wait_alone(sp, o1_ready, g)
                    for b in range(PAIR):
                        sp.dma_start(w_tok[:, b, :], w_row[b * HEADS:(b + 1) * HEADS]).then_inc(w_spread, 16)
                if active(i, EXPERTS):
                    g = i - EXPERTS
                    wait_alone(sp, first_summed, EX * (g + 1))
                    wait_alone(sp, second_summed, EX * (g + 1))
                    sp.dma_start(out_g[g], y).then_inc(stored, 16)
                if active(i, PROJECT):
                    g = i - PROJECT
                    relay_write(g, "q1", q_split, order(i, "q1") + 1)
                    relay_write(g, "k1", k_split, order(i, "k1") + 1)
                    relay_read(g, "q1", qs1, (0, 0, 1), self_scored)
                    relay_read(g, "k1", ks1_in, (0, 1, 0), k1_laid, 1)
                if active(i + 1, PROJECT) and not (isinstance(i, int) and i + 1 >= NG):
                    load_x(i + 1)
                if active(i, SELF):
                    relay_write(i - SELF, "q2", q_split, order(i, "q2") + 1)

            def load_x(g):
                wait_alone(sp, ln_done[0], g)
                wait_alone(sp, x_o1_ready, g)
                sp.dma_start(x_in[:], x_g[g]).then_inc(x_loaded, 16)

            for i in range(FIRST):
                iteration(i)
            with sp.Fori(FIRST, LAST - 1) as i:
                iteration(i)
            for i in range(LAST - 1, NG + STAGES - 1):
                iteration(i)
            sp.wait_ge(stored, 16 * NG)

        @block.gpsimd
        def _(pool):
            for m in (ident, ident_bf, mask_bf):
                nc.gpsimd.memset(m[:], 0.0).then_inc(ident_zero, 1)
            pool.wait_ge(ident_zero, 3)
            for m in (ident, ident_bf):
                nc.gpsimd.affine_select(out=m[:], in_=m[:], compare_op=ALU.not_equal, fill=1.0, base=0,
                                        pattern=[[-1, P]], channel_multiplier=1).then_inc(ident_ready, 1)
            nc.gpsimd.affine_select(out=mask_bf[:], in_=mask_bf[:], compare_op=ALU.is_ge, fill=MASKED,
                                    base=WINDOW // 2, pattern=[[-1, P]], channel_multiplier=1).then_inc(mask_ready, 1)
            pool.wait_ge(mask_ready, 1)
            nc.gpsimd.affine_select(out=mask_bf[:], in_=mask_bf[:], compare_op=ALU.is_ge, fill=MASKED,
                                    base=WINDOW // 2, pattern=[[1, P]], channel_multiplier=-1).then_inc(mask_ready, 1)
            for s in (qs1, ks2):
                nc.gpsimd.memset(s[:].bitcast(F32), 0.0).then_inc(zeros_ready, 1)
            for e in range(EX):
                nc.gpsimd.memset(falling[:, :, e:e + 1], float(EX - e)).then_inc(falling_ready, 1)
            nc.gpsimd.memset(minus_half[:], -0.5).then_inc(falling_ready, 1)
            pool.wait_ge(falling_ready, EX + 1)
            pool.wait_ge(bias_in, 8 * 16)

            def norm(k, g, source, drained):
                wait_alone(pool, ln_moments[k], g + 1)
                nc.gpsimd.tensor_scalar(rstd[k][:], moments[k][:, :, 1], EPS, None, ALU.add).then_inc(ln_rstd[k], 1)
                pool.wait_ge(ln_rstd[k], 2 * g + 1)
                nc.gpsimd.tensor_tensor(rstd[k][:], rstd[k][:], minus_half[:], ALU.pow).then_inc(ln_rstd[k], 1)
                wait_alone(pool, ln_rstd[k], 2 * g + 2)
                wait_alone(pool, bank_filled, drained)
                for b in range(PAIR):
                    last = nc.gpsimd.tensor_scalar(h[k][:, b, :], source[:, b, :], moments[k][:, b, 0:1],
                                                   rstd[k][:, b:b + 1], ALU.subtract, ALU.mult)
                last.then_inc(ln_done[k], 1)

            def turned_before(i, name, stage):
                return order(i - 1, name) + 1 if active(i - 1, stage) and not (isinstance(i, int) and i == stage) else 0

            def add_bias(to, source, n):
                return nc.gpsimd.tensor_tensor(
                    to[:], source[:], brow[:, R_AT[n], :].unsqueeze(1).to_broadcast([P, PAIR, D]), ALU.add)

            def iteration(i):
                if active(i, EXPERTS):
                    norm(2, i - EXPERTS, x2, turned_before(i, "turn_h3", EXPERTS))
                if active(i, CROSS):
                    g = i - CROSS
                    pool.wait_ge(x1_ready, g + 1)
                    wait(pool, x2_ready, g)
                    add_bias(x1_o2, x1, "o2").then_inc(x1_o2_ready, 1)
                if active(i, PROJECT):
                    norm(0, i - PROJECT, x_in, turned_before(i, "turn_h1", PROJECT))
                if active(i, EXPERTS):
                    g = i - EXPERTS
                    for e in range(EX):
                        pool.wait_ge(second_scaled, EX * g + e + 1)
                        if e:
                            pool.wait_ge(second_summed, EX * g + e)
                        nc.gpsimd.tensor_tensor(y[:, 1, :], y[:, 1, :], scaled[:, e % 4, :] if e else x2[:, 1, :], ALU.add)\
                            .then_inc(second_summed, 1)
                if active(i, SELF):
                    g = i - SELF
                    pool.wait_ge(w_spread, 2 * 16 * (g + 1))
                    wait(pool, bank_filled, turned_before(i, "turn_o1", SELF))
                    nc.gpsimd.tensor_tensor(
                        o1[:].rearrange("p b (g x) -> p (b g) x", x=HD),
                        v1[:].rearrange("p b (g x) -> p (b g) x", x=HD),
                        w_tok[:].rearrange("p b g -> p (b g)").unsqueeze(2).to_broadcast([P, PAIR * HEADS, HD]),
                        ALU.mult).then_inc(o1_ready, 1)
                    norm(1, g, x1, turned_before(i, "turn_h2", SELF))
                if active(i, PROJECT):
                    g = i - PROJECT
                    pool.wait_ge(x_loaded, 16 * (g + 1))
                    wait(pool, x1_ready, g)
                    add_bias(x_o1, x_in, "o1").then_inc(x_o1_ready, 1)

            pipeline(pool, iteration)

        @block.scalar
        def _(act):
            act.wait_ge(weights_in, 8 * 16)
            for n in names:
                nc.scalar.activation(W[n][:, 0], w_raw[n], ACT.Copy, scale=w_scale[n]).then_inc(w_high, 1)
            act.wait_ge(experts_in, C * 16)
            for c in range(C):
                nc.scalar.activation(WE[:, 0, c, :], e_raw[:, c, :], ACT.Copy).then_inc(w_high, 1)
            act.wait_ge(w_low, 8 + C)
            act.wait_ge(bcol_ready, 4)

            def high(i, name, target):
                act.wait_ge(bank_filled, order(i, name) + 1)
                nc.scalar.activation(target[:, 0].rearrange("p c t -> p (c t)"), bank[:, bank_of(name), :], ACT.Copy)\
                    .then_inc(bank_rounded, 1)

            def high_biased(i, name, target):
                act.wait_ge(bank_filled, order(i, name) + 1)
                for c in range(C):
                    last = nc.scalar.activation(target[:, 0, c, :], bank[:, bank_of(name), c * TOK2:(c + 1) * TOK2],
                                                ACT.Identity, bias=bcol[:, B_AT[name], c:c + 1])
                last.then_inc(bank_rounded, 1)

            def exps(maxed, exped, g, u, nmax, e, total):
                act.wait_ge(maxed, UNITS * g + u + 1)
                for hh in range(2):
                    for b in range(PAIR):
                        col = (hh * PAIR + b) * P
                        last = nc.scalar.activation(e[:, u % SLOTS, hh, b, :], scores[:, u % 2, col:col + P], ACT.Exp,
                                                    bias=nmax[:, u, hh * PAIR + b:hh * PAIR + b + 1],
                                                    accum_out=total[:, b, 2 * u + hh:2 * u + hh + 1])
                last.then_inc(exped, 1)

            def iteration(i):
                gp, gs, gc, ge = i - PROJECT, i - SELF, i - CROSS, i - EXPERTS

                def self_exps(u):
                    if active(i, SELF):
                        wait(act, self_weighed, UNITS * gs + u + 1 - SLOTS)
                        exps(self_maxed, self_exped, gs, u, nmax1, e1, sum1)

                def cross_exps(u):
                    if active(i, CROSS):
                        wait(act, cross_turned, UNITS * gc + u + 1 - SLOTS)
                        exps(cross_maxed, cross_exped, gc, u, nmax2, e2, sum2)

                def copy_turned(u):
                    if active(i, CROSS):
                        act.wait_ge(cross_turned, UNITS * gc + u + 1)
                        wait(act, cross_attended, UNITS * gc + u - 1)
                        nc.scalar.activation(e2_t[:, 0].rearrange("p h b a -> p (h b a)"), turned_e[:], ACT.Copy)\
                            .then_inc(e2_by_act, 1)

                def scale_second(q):
                    if not active(i, EXPERTS):
                        return
                    act.wait_ge(expert_ready, FUNITS * ge + 2 * q + 2)
                    for e in (2 * q, 2 * q + 1):
                        source = attended[:, (e % 2) * D:(e % 2 + 1) * D]
                        if e == 0:
                            ins = nc.scalar.activation(y[:, 1, :], source, ACT.Identity,
                                                       bias=r_bias[:, 1:2], scale=r_c[:, 1, 0:1])
                        else:
                            wait(act, second_summed, EX * ge + (e - 3 if e > 4 else 0))
                            ins = nc.scalar.activation(scaled[:, e % 4, :], source, ACT.Copy, scale=r_c[:, 1, e:e + 1])
                        ins.then_inc(second_scaled, 1)

                def first_base():
                    if active(i, EXPERTS):
                        act.wait_ge(routed, ge + 1)
                        wait(act, stored, 16 * ge)
                        nc.scalar.activation(y[:, 0, :], x2[:, 0, :], ACT.Identity, bias=r_bias[:, 0:1])\
                            .then_inc(base_ready, 1)

                def router_exps():
                    if active(i, EXPERTS):
                        act.wait_ge(r_maxed, ge + 1)
                        for b in range(PAIR):
                            last = nc.scalar.activation(r_exp[:, b, :], logits[:, b, :], ACT.Exp, bias=r_nmax[:, b:b + 1],
                                                        accum_out=r_sum[:, b:b + 1])
                        last.then_inc(r_exped, 1)

                if active(i, EXPERTS):
                    high(i, "turn_o2", turned_o)
                self_exps(0)
                if active(i, CROSS):
                    high(i, "turn_ctx", turned_in)
                self_exps(1)
                if active(i, CROSS):
                    wait(act, relay_in["k1"], 16 * min(i, NG) if isinstance(i, int) else 16 * i)
                    high_biased(i, "k2", k_split)
                self_exps(2)
                if active(i, EXPERTS):
                    high(i, "turn_h3", turned_h)
                self_exps(3)
                router_exps()
                self_exps(4)
                self_exps(5)
                first_base()
                self_exps(6)
                scale_second(0)
                self_exps(7)
                for q in range(1, EX // 2):
                    scale_second(q)
                cross_exps(0)
                if active(i, PROJECT):
                    high(i, "turn_h1", turned_in)
                cross_exps(1)
                copy_turned(0)
                if active(i, PROJECT):
                    if active(i - 1, SELF):
                        wait(act, relay_in["q2"], 16 * (i - 1))
                    high_biased(i, "q1", q_split)
                cross_exps(2)
                if active(i, PROJECT):
                    if active(i, CROSS):
                        act.wait_ge(relay_in["k2"], 16 * (gc + 1))
                    high_biased(i, "k1", k_split)
                cross_exps(3)
                copy_turned(2)
                if active(i, SELF):
                    high(i, "turn_o1", turned_o)
                cross_exps(4)
                cross_exps(5)
                copy_turned(4)
                cross_exps(6)
                if active(i, SELF):
                    high(i, "turn_h2", turned_h)
                cross_exps(7)
                copy_turned(6)
                if active(i, SELF):
                    wait(act, relay_in["q2"], 16 * gs)
                    if active(i, PROJECT):
                        act.wait_ge(relay_in["q1"], 16 * (gp + 1))
                    high_biased(i, "q2", q_split)

            pipeline(act, iteration)

        @block.vector
        def _(dve):
            dve.wait_ge(bias_in, 8 * 16)
            for n in b_dram:
                nc.vector.tensor_scalar(bcol[:, B_AT[n], :], bcol_raw[:, B_AT[n], :], w_scale[n], None, ALU.mult)\
                    .then_inc(bcol_ready, 1)
            dve.wait_ge(bcol_ready, 4)
            for k, n in enumerate(names):
                dve.wait_ge(w_high, k + 1)
                nc.vector.scalar_tensor_tensor(out=W[n][:, 1], in0=w_raw[n], scalar=w_scale[n], in1=W[n][:, 0],
                                               op0=ALU.mult, op1=ALU.subtract).then_inc(w_low, 1)
            for c in range(C):
                dve.wait_ge(w_high, 8 + c + 1)
                nc.vector.tensor_tensor(WE[:, 1, c, :], e_raw[:, c, :], WE[:, 0, c, :], ALU.subtract).then_inc(w_low, 1)
            dve.wait_ge(router_turned, 1)
            nc.vector.tensor_copy(router_t[:], router_ps).then_inc(router_ready, 1)
            dve.wait_ge(falling_ready, EX)

            def low(i, name, target):
                dve.wait_ge(bank_rounded, order(i, name, rounded=True) + 1)
                nc.vector.tensor_tensor(target[:, 1].rearrange("p c t -> p (c t)"), bank[:, bank_of(name), :],
                                        target[:, 0].rearrange("p c t -> p (c t)"), ALU.subtract)\
                    .then_inc(bank_emptied, 1)

            def low_biased(i, name, target):
                dve.wait_ge(bank_rounded, order(i, name, rounded=True) + 1)
                for c in range(C):
                    last = nc.vector.scalar_tensor_tensor(
                        out=target[:, 1, c, :], in0=bank[:, bank_of(name), c * TOK2:(c + 1) * TOK2],
                        scalar=bcol[:, B_AT[name], c:c + 1], in1=target[:, 0, c, :], op0=ALU.add, op1=ALU.subtract)
                last.then_inc(bank_emptied, 1)

            def statistics(k, g, source):
                for b in range(PAIR):
                    last = nc.vector.bn_stats(stats[k][:, b, :], source[:, b, :])
                last.then_inc(ln_stats[k], 1)
                wait_alone(dve, ln_done[k], g)
                wait_alone(dve, ln_stats[k], g + 1)
                for b in range(PAIR):
                    last = nc.vector.bn_aggr(moments[k][:, b, :], stats[k][:, b, :])
                last.then_inc(ln_moments[k], 1)

            def maxima(scored, maxed, g, u, nmax):
                dve.wait_ge(scored, UNITS * g + u + 1)
                nc.vector.tensor_reduce(nmax[:, u, :], scores[:, u % 2, :].rearrange("p (s a) -> p s a", a=P), AX.X,
                                        ALU.max, negate=True).then_inc(maxed, 1)

            def in_bank(name):
                return bank[:, bank_of(name), :].rearrange("p (b n) -> p b n", b=PAIR)

            def with_bias(i, name, to, done):
                dve.wait_ge(bank_filled, order(i, name) + 1)
                wait(dve, *done)
                nc.vector.tensor_tensor(to[:], in_bank(name),
                                        brow[:, R_AT[name], :].unsqueeze(1).to_broadcast([P, PAIR, D]), ALU.add)\
                    .then_inc(bank_emptied, 1)

            def iteration(i):
                gp, gs, gc, ge = i - PROJECT, i - SELF, i - CROSS, i - EXPERTS

                def self_max(u):
                    if active(i, SELF):
                        maxima(self_scored, self_maxed, gs, u, nmax1)

                def self_invert(u):
                    if active(i, SELF):
                        dve.wait_ge(self_exped, UNITS * gs + u + 1)
                        nc.vector.reciprocal(rsum1[:, :, 2 * u:2 * u + 2], sum1[:, :, 2 * u:2 * u + 2])\
                            .then_inc(self_inverted, 1)

                def cross_max(u):
                    if active(i, CROSS):
                        maxima(cross_scored, cross_maxed, gc, u, nmax2)

                def copy_turned(u):
                    if active(i, CROSS):
                        dve.wait_ge(cross_turned, UNITS * gc + u + 1)
                        wait(dve, cross_attended, UNITS * gc + u - 1)
                        nc.vector.tensor_copy(e2_t[:, 1].rearrange("p h b a -> p (h b a)"), turned_e[:])\
                            .then_inc(e2_by_dve, 1)

                def sum_first(q):
                    if not active(i, EXPERTS):
                        return
                    dve.wait_ge(expert_ready, FUNITS * ge + 2 * q + 1)
                    for e in (2 * q, 2 * q + 1):
                        if e == 0:
                            dve.wait_ge(base_ready, ge + 1)
                        else:
                            dve.wait_ge(first_summed, EX * ge + e)
                        nc.vector.scalar_tensor_tensor(
                            out=y[:, 0, :], in0=turned_e[:, (e % 2) * D:(e % 2 + 1) * D], scalar=r_c[:, 0, e:e + 1],
                            in1=y[:, 0, :], op0=ALU.mult, op1=ALU.add).then_inc(first_summed, 1)

                STEPS = 18
                done = [0]

                def step(ins):
                    done[0] += 1
                    ins.then_inc(r_step, 1)
                    dve.wait_ge(r_step, STEPS * ge + done[0])

                def wide(a, n):
                    return a.unsqueeze(2).to_broadcast([P, PAIR, n])

                def router_max():
                    if active(i, EXPERTS):
                        dve.wait_ge(logits_ready, ge + 1)
                        nc.vector.tensor_reduce(r_nmax[:], logits, AX.X, ALU.max, negate=True).then_inc(r_maxed, 1)

                def route():
                    if not active(i, EXPERTS):
                        return
                    dve.wait_ge(r_exped, ge + 1)
                    step(nc.vector.reciprocal(r_rsum[:], r_sum[:]))
                    step(nc.vector.tensor_tensor(r_p[:], r_exp[:], wide(r_rsum[:], EX), ALU.mult))
                    p = r_p
                    for j in range(2):
                        step(nc.vector.tensor_reduce(r_top[:, :, j], p[:], AX.X, ALU.max))
                        step(nc.vector.tensor_tensor(r_eq[:], p[:], wide(r_top[:, :, j], EX), ALU.is_equal))
                        step(nc.vector.tensor_tensor(r_key[:], r_eq[:], falling[:], ALU.mult))
                        step(nc.vector.tensor_reduce(r_first[:], r_key[:], AX.X, ALU.max))
                        step(nc.vector.tensor_tensor(r_hot[j][:], falling[:], wide(r_first[:], EX), ALU.is_equal))
                        if j == 0:
                            step(nc.vector.scalar_tensor_tensor(out=r_rest[:], in0=r_hot[0][:], scalar=-2.0, in1=r_p[:],
                                                                op0=ALU.mult, op1=ALU.add))
                            p = r_rest
                    step(nc.vector.scalar_tensor_tensor(out=r_norm[:], in0=r_top[:, :, 0], scalar=TOP_EPS,
                                                        in1=r_top[:, :, 1], op0=ALU.add, op1=ALU.add))
                    step(nc.vector.reciprocal(r_rnorm[:], r_norm[:]))
                    step(nc.vector.tensor_tensor(r_w[:], r_top[:], wide(r_rnorm[:], 2), ALU.mult))
                    nc.vector.tensor_tensor(r_wh[0][:], r_hot[0][:], wide(r_w[:, :, 0], EX), ALU.mult)
                    nc.vector.tensor_tensor(r_wh[1][:], r_hot[1][:], wide(r_w[:, :, 1], EX), ALU.mult)
                    step(nc.vector.tensor_tensor(r_pw[:], r_top[:], r_w[:], ALU.mult))
                    nc.vector.tensor_reduce(r_bias[:], r_pw[:], AX.X, ALU.add)
                    step(nc.vector.tensor_tensor(r_c[:], r_wh[0][:], r_wh[1][:], ALU.add))
                    assert done[0] == STEPS, done
                    nc.vector.tensor_copy(r_key[:, :, 0:1], r_c[:, :, 0:1]).then_inc(routed, 1)

                if active(i, EXPERTS):
                    low(i, "turn_o2", turned_o)
                self_max(0)
                self_max(1)
                if active(i, CROSS):
                    low(i, "turn_ctx", turned_in)
                if active(i, EXPERTS):
                    dve.wait_ge(bank_filled, order(i, "out2") + 1)
                    dve.wait_ge(x1_o2_ready, ge + 1)
                    wait(dve, ln_done[2], ge)
                    nc.vector.tensor_tensor(x2[:], in_bank("out2"), x1_o2[:], ALU.add).then_inc(bank_emptied, 1)
                    dve.wait_ge(bank_emptied, order(i, "out2") + 1)
                    for b in range(PAIR):
                        last = nc.vector.bn_stats(stats[2][:, b, :], x2[:, b, :])
                    last.then_inc(x2_ready, 1)
                    wait_alone(dve, x2_ready, ge + 1)
                    for b in range(PAIR):
                        last = nc.vector.bn_aggr(moments[2][:, b, :], stats[2][:, b, :])
                    last.then_inc(ln_moments[2], 1)
                self_max(2)
                self_invert(0)
                if active(i, CROSS):
                    low_biased(i, "k2", k_split)
                self_max(3)
                self_invert(1)
                if active(i, CROSS):
                    with_bias(i, "v2", v2, (cross_attended, UNITS * gc))
                if active(i, EXPERTS):
                    low(i, "turn_h3", turned_h)
                self_max(4)
                self_invert(2)
                router_max()
                self_max(5)
                self_invert(3)
                if active(i, PROJECT):
                    dve.wait_ge(x_loaded, 16 * (gp + 1))
                    statistics(0, gp, x_in)
                route()
                self_max(6)
                self_invert(4)
                sum_first(0)
                self_max(7)
                self_invert(5)
                sum_first(1)
                self_invert(6)
                sum_first(2)
                self_invert(7)
                sum_first(3)
                if active(i, SELF):
                    dve.wait_ge(self_weighed, UNITS * (gs + 1))
                    if isinstance(i, int) and gs == 0:
                        pass
                    else:
                        dve.wait_ge(bank_filled, order(i - 1, "turn_w") + 1)
                    nc.vector.tensor_copy(w_col[:], w_sum).then_inc(w_copied, 1)

                cross_max(0)
                if active(i, SELF):
                    dve.wait_ge(bank_filled, order(i, "turn_w") + 1)
                    wait(dve, w_spread, 2 * 16 * gs)
                    nc.vector.tensor_copy(w_row[:], bank[0:PAIR * HEADS, bank_of("turn_w"), 0:P]
                                          .rearrange("p (g t) -> p t g", t=8)).then_inc(bank_emptied, 1)
                    dve.wait_ge(bank_emptied, order(i, "turn_w") + 1)
                    nc.vector.tensor_copy(r_key[0:1, 0, 0:1], w_row[0:1, 0, 0:1]).then_inc(w_row_ready, 1)
                if active(i, PROJECT):
                    low(i, "turn_h1", turned_in)
                cross_max(1)
                if active(i, PROJECT):
                    low_biased(i, "q1", q_split)
                cross_max(2)
                copy_turned(1)
                if active(i, PROJECT):
                    low_biased(i, "k1", k_split)
                cross_max(3)
                if active(i, SELF):
                    low(i, "turn_o1", turned_o)
                if active(i, PROJECT):
                    with_bias(i, "v1", v1, (o1_ready, gp))
                cross_max(4)
                copy_turned(3)
                if active(i, SELF):
                    dve.wait_ge(bank_filled, order(i, "out1") + 1)
                    dve.wait_ge(x_o1_ready, gs + 1)
                    wait(dve, x1_o2_ready, gs)
                    wait(dve, ln_done[1], gs)
                    nc.vector.tensor_tensor(x1[:], in_bank("out1"), x_o1[:], ALU.add).then_inc(bank_emptied, 1)
                    dve.wait_ge(bank_emptied, order(i, "out1") + 1)
                    for b in range(PAIR):
                        last = nc.vector.bn_stats(stats[1][:, b, :], x1[:, b, :])
                    last.then_inc(x1_ready, 1)
                    wait_alone(dve, x1_ready, gs + 1)
                    for b in range(PAIR):
                        last = nc.vector.bn_aggr(moments[1][:, b, :], stats[1][:, b, :])
                    last.then_inc(ln_moments[1], 1)
                cross_max(5)
                cross_max(6)
                copy_turned(5)
                if active(i, SELF):
                    low(i, "turn_h2", turned_h)
                cross_max(7)
                copy_turned(7)
                if active(i, CROSS):
                    dve.wait_ge(cross_exped, UNITS * (gc + 1))
                    nc.vector.reciprocal(rsum2[:], sum2[:]).then_inc(cross_inverted, 1)
                    dve.wait_ge(cross_inverted, gc + 1)
                    dve.wait_ge(cross_attended, UNITS * (gc + 1))
                    if active(i, EXPERTS):
                        dve.wait_ge(bank_filled, order(i, "turn_o2") + 1)
                    nc.vector.tensor_tensor(
                        o2[:].rearrange("p b (g x) -> p (b g) x", x=HD),
                        attended[:].rearrange("p (s x) -> p s x", x=HD),
                        rsum2[:].rearrange("p b g -> p (b g)").unsqueeze(2).to_broadcast([P, PAIR * HEADS, HD]),
                        ALU.mult).then_inc(o2_ready, 1)
                if active(i, SELF):
                    low_biased(i, "q2", q_split)
                if active(i, PROJECT):
                    dve.wait_ge(relay_out["k1"], 6 * 16 * (gp + 1))
                    wait(dve, self_scored, UNITS * gp)
                    nc.vector.tensor_copy(ks1[:].rearrange("r e (g t) -> r e g t", t=8),
                                          ks1_in[:].rearrange("r g (e t) -> r e g t", t=8)).then_inc(k1_laid, 1)

            pipeline(dve, iteration)

        @block.tensor
        def _(pe):
            pe.wait_ge(ident_ready, 2)
            pe.wait_ge(router_in, 16)
            for c in range(C):
                last = nc.tensor.transpose(router_ps[:, c, :], router_raw[:, c * P:(c + 1) * P], ident[0:EX, 0:EX])
            last.then_inc(router_turned, 1)
            pe.wait_ge(router_ready, 1)
            pe.wait_ge(w_low, 8 + C)
            pe.wait_ge(mask_ready, 2)

            PRODUCTS = ((0, 0), (0, 1), (1, 0))

            def turn(i, name, source):
                wait(pe, bank_emptied, emptied_before(i, name))
                for c in range(C):
                    for b in range(PAIR):
                        last = nc.tensor.transpose(bank[:, bank_of(name), (c * PAIR + b) * P:(c * PAIR + b + 1) * P],
                                                   source[:, b, c * P:(c + 1) * P], ident[:])
                last.then_inc(bank_filled, 1)

            def project_turned(i, name, weights, turned):
                wait(pe, bank_emptied, emptied_before(i, name))
                for m in range(C):
                    for k, (wp, xp) in enumerate(PRODUCTS):
                        for c in range(C):
                            last = nc.tensor.matmul(
                                bank[:, bank_of(name), m * TOK2:(m + 1) * TOK2], weights[:, wp, c, m * P:(m + 1) * P],
                                turned[:, xp, c, :], start=(k == 0 and c == 0), stop=(k == 2 and c == C - 1))
                last.then_inc(bank_filled, 1)

            def project(i, name, weights, turned):
                wait(pe, bank_emptied, emptied_before(i, name))
                for b in range(PAIR):
                    for k, (wp, xp) in enumerate(PRODUCTS):
                        for c in range(C):
                            last = nc.tensor.matmul(
                                bank[:, bank_of(name), b * D:(b + 1) * D], turned[:, xp, c, b * TOK:(b + 1) * TOK],
                                weights[:, wp, c, :], start=(k == 0 and c == 0), stop=(k == 2 and c == C - 1))
                last.then_inc(bank_filled, 1)

            def iteration(i):
                gp, gs, gc, ge = i - PROJECT, i - SELF, i - CROSS, i - EXPERTS

                def self_scores(u):
                    if not active(i, SELF):
                        return
                    if u == 0:
                        pe.wait_ge(relay_out["q1"], 6 * 16 * (gs + 1))
                        pe.wait_ge(k1_laid, gs + 1)
                    wait(pe, self_exped, UNITS * gs + u - 1)
                    if u < 2:
                        wait(pe, cross_exped, UNITS * (gs - 1))
                    for hh in range(2):
                        e = 2 * u + hh
                        t = 8 * e
                        last = nc.tensor.matmul(scores[:, u % 2, hh * TOK2:(hh + 1) * TOK2],
                                                ks1[:, e, :], qs1[:, :, :, t:t + 8], start=True, stop=True)
                    last.then_inc(self_scored, 1)

                def self_weights(u):
                    if not active(i, SELF):
                        return
                    pe.wait_ge(self_inverted, UNITS * gs + u + 1)
                    if u == 0:
                        wait(pe, w_copied, gs)
                    for hh in range(2):
                        for b in range(PAIR):
                            e = 2 * u + hh
                            last = nc.tensor.matmul(w_sum[:, b * HEADS + e:b * HEADS + e + 1], e1[:, u % SLOTS, hh, b, :],
                                                    rsum1[:, b, e:e + 1], start=True, stop=True)
                    last.then_inc(self_weighed, 1)

                def cross_scores(u):
                    if not active(i, CROSS):
                        return
                    if u == 0:
                        pe.wait_ge(relay_out["q2"], 6 * 16 * (gc + 1))
                        pe.wait_ge(relay_out["k2"], 6 * 16 * (gc + 1))
                    wait(pe, cross_exped, UNITS * gc + u - 1)
                    if u < 2:
                        wait(pe, self_exped, UNITS * (min(gc + 2, NG) if isinstance(i, int) else gc + 2))
                    nc.tensor.matmul(scores[:, u % 2, :], ident_bf[:], mask_bf[:].unsqueeze(1).to_broadcast([P, 4, P]),
                                     start=True, stop=False, skip_group_check=True)
                    for hh in range(2):
                        e = 2 * u + hh
                        last = nc.tensor.matmul(scores[:, u % 2, hh * TOK2:(hh + 1) * TOK2], qs2[:, e, :],
                                                ks2[:, :, e, :], start=False, stop=True, skip_group_check=True)
                    last.then_inc(cross_scored, 1)

                def cross_turn(u):
                    if not active(i, CROSS):
                        return
                    pe.wait_ge(cross_exped, UNITS * gc + u + 1)
                    if u == 0:
                        wait(pe, first_summed, EX * gc)
                        wait(pe, e2_by_dve, UNITS // 2 * gc)
                    elif u % 2:
                        pe.wait_ge(e2_by_act, UNITS // 2 * gc + u // 2 + 1)
                    else:
                        pe.wait_ge(e2_by_dve, UNITS // 2 * gc + u // 2)
                    for hh in range(2):
                        for b in range(PAIR):
                            col = (hh * PAIR + b) * P
                            last = nc.tensor.transpose(turned_e[:, col:col + P], e2[:, u % SLOTS, hh, b, :], ident[:])
                    last.then_inc(cross_turned, 1)

                def cross_attend(u):
                    if not active(i, CROSS):
                        return
                    if u == 0:
                        pe.wait_ge(bank_emptied, order(i, "v2") + 1)
                        wait(pe, second_scaled, EX * gc)
                    pe.wait_ge(*((e2_by_dve, UNITS // 2 * gc + u // 2 + 1) if u % 2 else
                                 (e2_by_act, UNITS // 2 * gc + u // 2 + 1)))
                    for hh in range(2):
                        for b in range(PAIR):
                            e = 2 * u + hh
                            at = (b * HEADS + e) * HD
                            last = nc.tensor.matmul(attended[:, at:at + HD], e2_t[:, u % 2, hh, b, :],
                                                    v2[:, b, e * HD:(e + 1) * HD], start=True, stop=True)
                    last.then_inc(cross_attended, 1)

                def route():
                    if not active(i, EXPERTS):
                        return
                    pe.wait_ge(bank_emptied, order(i, "turn_h3") + 1)
                    wait(pe, r_exped, ge)
                    for b in range(PAIR):
                        for k in range(2 * C):
                            last = nc.tensor.matmul(logits[:, b, :],
                                                    turned_h[:, k // C, k % C, b * TOK:(b + 1) * TOK].bitcast(F32),
                                                    router_t[:, k % C, :], start=(k == 0), stop=(k == 2 * C - 1))
                    last.then_inc(logits_ready, 1)

                def expert_pair(f):
                    if not active(i, EXPERTS):
                        return
                    if f >= PAIR:
                        pe.wait_ge((first_summed, second_scaled)[f % 2], EX * ge + 2 * (f // 2))
                    elif f == 0:
                        pe.wait_ge(e2_by_dve, UNITS // 2 * (ge + 1))
                    else:
                        pe.wait_ge(r_exped, ge + 1)
                    b, col = f % PAIR, (f // PAIR) * 2 * D
                    for k, (wp, xp) in enumerate(PRODUCTS):
                        for c in range(C):
                            last = nc.tensor.matmul((turned_e, attended)[f % 2][:],
                                                    turned_h[:, xp, c, b * TOK:(b + 1) * TOK], WE[:, wp, c, col:col + 2 * D],
                                                    start=(k == 0 and c == 0), stop=(k == 2 and c == C - 1))
                    last.then_inc(expert_ready, 1)

                if active(i, EXPERTS):
                    pe.wait_ge(o2_ready, ge + 1)
                    turn(i, "turn_o2", o2)
                self_scores(0)
                self_scores(1)
                if active(i, CROSS):
                    pe.wait_ge(c_loaded, 16 * (gc + 1))
                    turn(i, "turn_ctx", c_in)
                if active(i, EXPERTS):
                    pe.wait_ge(bank_emptied, order(i, "turn_o2") + 1)
                    project(i, "out2", W["o2"], turned_o)
                self_scores(2)
                if active(i, CROSS):
                    pe.wait_ge(bank_emptied, order(i, "turn_ctx") + 1)
                    project_turned(i, "k2", W["k2"], turned_in)
                self_weights(0)
                self_scores(3)
                if active(i, CROSS):
                    project(i, "v2", W["v2"], turned_in)
                self_weights(1)
                if active(i, EXPERTS):
                    pe.wait_ge(ln_done[2], ge + 1)
                    turn(i, "turn_h3", h[2])
                self_scores(4)
                self_weights(2)
                route()
                self_scores(5)
                expert_pair(0)
                self_weights(3)
                self_scores(6)
                expert_pair(1)
                self_weights(4)
                self_scores(7)
                expert_pair(2)
                self_weights(5)
                expert_pair(3)
                self_weights(6)
                expert_pair(4)
                self_weights(7)
                for f in range(5, FUNITS):
                    expert_pair(f)

                cross_scores(0)
                cross_scores(1)
                if active(i, SELF):
                    pe.wait_ge(w_copied, gs + 1)
                    wait(pe, bank_emptied, emptied_before(i, "turn_w"))
                    nc.tensor.transpose(bank[0:PAIR * HEADS, bank_of("turn_w"), 0:P], w_col[:], ident[:])\
                        .then_inc(bank_filled, 1)
                if active(i, PROJECT):
                    pe.wait_ge(ln_done[0], gp + 1)
                    turn(i, "turn_h1", h[0])
                cross_turn(0)
                cross_scores(2)
                if active(i, PROJECT):
                    pe.wait_ge(bank_emptied, order(i, "turn_h1") + 1)
                    project_turned(i, "q1", W["q1"], turned_in)
                cross_turn(1)
                cross_attend(0)
                cross_scores(3)
                if active(i, PROJECT):
                    project_turned(i, "k1", W["k1"], turned_in)
                cross_turn(2)
                cross_attend(1)
                cross_scores(4)
                if active(i, SELF):
                    pe.wait_ge(o1_ready, gs + 1)
                    turn(i, "turn_o1", o1)
                cross_turn(3)
                cross_attend(2)
                if active(i, PROJECT):
                    project(i, "v1", W["v1"], turned_in)
                cross_scores(5)
                cross_turn(4)
                cross_attend(3)
                if active(i, SELF):
                    pe.wait_ge(bank_emptied, order(i, "turn_o1") + 1)
                    project(i, "out1", W["o1"], turned_o)
                cross_scores(6)
                cross_turn(5)
                cross_attend(4)
                cross_scores(7)
                cross_turn(6)
                cross_attend(5)
                if active(i, SELF):
                    pe.wait_ge(ln_done[1], gs + 1)
                    turn(i, "turn_h2", h[1])
                cross_turn(7)
                cross_attend(6)
                cross_attend(7)
                if active(i, SELF):
                    pe.wait_ge(bank_emptied, order(i, "turn_h2") + 1)
                    project_turned(i, "q2", W["q2"], turned_h)

            pipeline(pe, iteration)


_INS = ["x", "ctx_1024"] + [f"L0_{a}_{w}" for a in ("attn", "xattn")
                            for w in ("Wq", "bq", "Wk", "bk", "Wv", "bv", "Wo", "bo")] \
    + ["L0_ffn_router_w", "L0_ffn_expert_weights"]


def kernel(**inputs):
    import numpy as _np
    import concourse.bacc as _bacc
    from concourse import mybir as _mybir
    from concourse.bass_utils import run_bass_kernel_spmd as _run

    nc = _bacc.Bacc("TRN2", target_bir_lowering=False, num_devices=1)
    arrays, args = {}, []
    for name in _INS:
        a = _np.ascontiguousarray(inputs[name])
        arrays[f"in_{name}"] = a
        args.append(nc.dram_tensor(f"in_{name}", a.shape, _mybir.dt.from_np(a.dtype), kind="ExternalInput").ap())
    shape = inputs["x"].shape
    args.append(nc.dram_tensor("out_0", shape, _mybir.dt.float32, kind="ExternalOutput").ap())
    decoder_layer(nc, *args)
    r = _run(nc, [arrays], core_ids=[0])
    return r.results[0]["out_0"]
```

```python
from contextlib import ExitStack

import concourse.bass as bass
from concourse import mybir

F32 = mybir.dt.float32
F32R = mybir.dt.float32r
BF16 = mybir.dt.bfloat16
ACT = mybir.ActivationFunctionType
ALU = mybir.AluOpType
AX = mybir.AxisListType

P = 128
EPS = 1e-5
TOP_EPS = 1e-6
WINDOW = 128
MASKED = -1e30
PAIR = 2

PROJECT, SELF, CROSS, EXPERTS = range(4)
STAGES = 4

BANK_USERS = [
    ("turn_ctx", CROSS, True), ("turn_o2", EXPERTS, True), ("turn_h2", CROSS, True),
    ("k2", CROSS, True), ("out2", EXPERTS, False), ("q2", CROSS, True),
    ("v2", CROSS, False), ("turn_h3", EXPERTS, True), ("turn_h1", PROJECT, True),
    ("k1", PROJECT, True), ("q1", PROJECT, True), ("v1", PROJECT, False),
    ("turn_o1", SELF, True), ("out1", SELF, False),
]
BANKS = 3


def decoder_layer(nc, x, ctx, wq1, bq1, wk1, bk1, wv1, bv1, wo1, bo1,
                  wq2, bq2, wk2, bk2, wv2, bv2, wo2, bo2, router, experts, out):
    BATCHES, TOK, D = x.shape
    EX = router.shape[0]
    HEADS = 16
    HD = D // HEADS
    C = D // P
    G = P // HD
    NG = BATCHES // PAIR
    ROWS = 3 * HD
    UNITS = HEADS // 2
    FUNITS = PAIR * EX // 2
    TOK2 = PAIR * TOK
    SCALE1 = float(D) ** -0.5
    SCALE2 = float(HD) ** -0.5
    assert TOK == P and D == C * P and BATCHES % PAIR == 0 and 2 * ROWS <= P and UNITS % 4 == 0
    FIRST, LAST = STAGES, NG
    SPLIT_AT = 0

    def active(i, stage):
        return not isinstance(i, int) or 0 <= i - stage < NG

    def order(i, name, rounded=False):
        users = [(n, s) for n, s, r in BANK_USERS if r or not rounded]
        at = [n for n, _ in users].index(name)
        if isinstance(i, int):
            return (sum(active(k, s) for k in range(i) for _, s in users)
                    + sum(active(i, s) for _, s in users[:at]))
        return order(FIRST, users[0][0], rounded) + len(users) * (i - FIRST) + at

    def bank_of(name):
        return [n for n, _, _ in BANK_USERS].index(name) % BANKS

    def emptied_before(i, name):
        if not isinstance(i, int):
            return order(i, name) - BANKS + 1
        at = [n for n, _, _ in BANK_USERS].index(name)
        before = [(k, p) for k in range(i + 1) for p, (_, s, _) in enumerate(BANK_USERS)
                  if (k, p) < (i, at) and p % BANKS == at % BANKS and active(k, s)]
        return order(before[-1][0], BANK_USERS[before[-1][1]][0]) + 1 if before else 0

    def wait(eng, sem, value):
        if not isinstance(value, int) or value > 0:
            eng.wait_ge(sem, value)

    def wait_alone(eng, sem, value):
        if not isinstance(value, int) or value > 0:
            eng.wait_ge(sem, value)
            eng.sem_inc(passed[eng.engine], 1)

    stack = ExitStack()
    with stack:
        def sb(name, shape, dt=F32):
            return stack.enter_context(nc.sbuf_tensor(name, shape, dt))

        def ps(name, shape):
            return stack.enter_context(nc.psum_tensor(name, shape, F32))

        def sem(name):
            return stack.enter_context(nc.semaphore(name))

        names = ["q1", "k1", "v1", "o1", "q2", "k2", "v2", "o2"]
        w_dram = dict(zip(names, [wq1, wk1, wv1, wo1, wq2, wk2, wv2, wo2]))
        w_scale = {n: {"q1": SCALE1, "k1": SCALE1, "q2": SCALE2}.get(n, 1.0) for n in names}
        W = {n: sb(f"w_{n}", [P, 2, C, D], F32R) for n in names}
        WE = sb("w_experts", [P, 2, C, EX * D], F32R)
        router_raw = sb("router_raw", [EX, D])
        router_t = sb("router_t", [P, C, EX])
        b_dram = {"q1": bq1, "k1": bk1, "q2": bq2, "k2": bk2}
        bcol_raw = sb("bcol_raw", [P, 4, C])
        bcol = sb("bcol", [P, 4, C])
        B_AT = {n: k for k, n in enumerate(b_dram)}
        brow = sb("brow", [P, 4, D])
        R_AT = {"v1": 0, "o1": 1, "v2": 2, "o2": 3}
        ident = sb("ident", [P, P])
        ident_bf = sb("ident_bf", [P, P], BF16)
        mask_bf = sb("mask_bf", [P, P], BF16)
        minus_half = sb("minus_half", [P, PAIR])
        falling = sb("falling", [P, PAIR, EX])

        x_in = sb("x_in", [P, PAIR, D])
        c_in = sb("c_in", [P, PAIR, D])
        x_o1 = sb("x_o1", [P, PAIR, D])
        x1 = sb("x1", [P, PAIR, D])
        x1_o2 = sb("x1_o2", [P, PAIR, D])
        x2 = sb("x2", [P, PAIR, D])
        h = [sb(f"h{k + 1}", [P, PAIR, D]) for k in range(3)]
        stats = [sb(f"stats{k + 1}", [P, PAIR, 6]) for k in range(3)]
        moments = [sb(f"moments{k + 1}", [P, PAIR, 2]) for k in range(3)]
        rstd = [sb(f"rstd{k + 1}", [P, PAIR]) for k in range(3)]
        v1 = sb("v1", [P, PAIR, D])
        v2 = sb("v2", [P, PAIR, D])
        o1 = sb("o1", [P, PAIR, D])
        o2 = sb("o2", [P, PAIR, D])
        turned_o = sb("turned_o", [P, 2, C, TOK2], F32R)
        turned_in = sb("turned_in", [P, 2, C, TOK2], F32R)
        turned_h = sb("turned_h", [P, 2, C, TOK2], F32R)
        q_split = sb("q_split", [P, 2, C, TOK2], F32R)
        k_split = sb("k_split", [P, 2, C, TOK2], F32R)
        ks1_in = sb("ks1_in", [PAIR * ROWS, HEADS, TOK], F32R)
        ks1 = sb("ks1", [PAIR * ROWS, HEADS, TOK], F32R)
        qs1 = sb("qs1", [PAIR * ROWS, PAIR, HEADS, TOK], F32R)
        qs2 = sb("qs2", [PAIR * ROWS, HEADS, TOK], F32R)
        ks2 = sb("ks2", [PAIR * ROWS, PAIR, HEADS, TOK], F32R)
        nmax1 = sb("nmax1", [P, UNITS, 4])
        nmax2 = sb("nmax2", [P, UNITS, 4])
        sum1 = sb("sum1", [P, PAIR, HEADS])
        sum2 = sb("sum2", [P, PAIR, HEADS])
        rsum1 = sb("rsum1", [P, PAIR * HEADS * (PAIR * HEADS + 1)])
        rsum1_places = rsum1[:].rearrange("p (b e k) -> p b e k", b=PAIR, e=HEADS)[:, :, :, 0]
        rsum2 = sb("rsum2", [P, PAIR, HEADS])
        w_row = sb("w_row", [PAIR * HEADS, 8, HEADS])
        w_tok = sb("w_tok", [P, PAIR, HEADS])
        r_nmax = sb("r_nmax", [P, PAIR])
        r_exp = sb("r_exp", [P, PAIR, EX])
        r_sum = sb("r_sum", [P, PAIR])
        r_rsum = sb("r_rsum", [P, PAIR])
        r_p = sb("r_p", [P, PAIR, EX])
        r_rest = sb("r_rest", [P, PAIR, EX])
        r_eq = sb("r_eq", [P, PAIR, EX])
        r_key = sb("r_key", [P, PAIR, EX])
        r_first = sb("r_first", [P, PAIR])
        r_hot = [sb(f"r_hot{j}", [P, PAIR, EX]) for j in range(2)]
        r_top = sb("r_top", [P, PAIR, 2])
        r_norm = sb("r_norm", [P, PAIR])
        r_rnorm = sb("r_rnorm", [P, PAIR])
        r_w = sb("r_w", [P, PAIR, 2])
        r_pw = sb("r_pw", [P, PAIR, 2])
        r_wh = [sb(f"r_wh{j}", [P, PAIR, EX]) for j in range(2)]
        r_c = sb("r_c", [P, PAIR, EX])
        r_bias = sb("r_bias", [P, PAIR])
        space = sb("space", [P, 7168])
        w_raw = {n: space[:, 512 * k:512 * k + 512].rearrange("p (c n) -> p c n", c=C)
                 for k, n in enumerate(names[:6])}
        w_raw.update({n: a[:] for n, a in zip(names[6:], h[1:])})
        e_raw = space[:, 3072:7168].rearrange("p (c n) -> p c n", c=C)
        SLOTS = 4
        e1 = space[:, 0:2048].rearrange("p (s h b a) -> p s h b a", s=SLOTS, h=2, b=PAIR)
        e2 = space[:, 2048:4096].rearrange("p (s h b a) -> p s h b a", s=SLOTS, h=2, b=PAIR)
        e2_t = space[:, 4096:5120].rearrange("p (s h b a) -> p s h b a", s=2, h=2, b=PAIR)
        scaled = space[:, 5120:6144].rearrange("p (s n) -> p s n", s=4)
        y = space[:, 6144:6656].rearrange("p (b n) -> p b n", b=PAIR)

        scores = ps("scores", [P, 2, 512])
        bank = ps("bank", [P, BANKS, 512])
        turned_e = ps("turned_e", [P, 512])
        attended = ps("attended", [P, 512])
        small = ps("small", [P, 512])
        w_sum = small[0:PAIR * HEADS, 0:P]
        logits = attended[:, 0:PAIR * EX].rearrange("p (b e) -> p b e", b=PAIR)
        router_ps = small[:, 128:128 + C * EX].rearrange("p (c e) -> p c e", c=C)

        relay = {n: nc.dram_tensor(f"relay_{n}", [3, HD, HEADS, PAIR, TOK], F32, kind="Internal").ap()
                 for n in ("q1", "k1", "q2", "k2")}
        RELAY_BOTH = {"q": 1, "k": 0}
        RELAY_HIGH = {"q": 0, "k": 2}

        weights_in, experts_in, bias_in, router_in = sem("weights_in"), sem("experts_in"), sem("bias_in"), sem("router_in")
        ident_zero, ident_ready, zeros_ready = sem("ident_zero"), sem("ident_ready"), sem("zeros_ready")
        mask_ready, falling_ready = sem("mask_ready"), sem("falling_ready")
        w_high, w_low, bcol_ready = sem("w_high"), sem("w_low"), sem("bcol_ready")
        router_turned, router_ready = sem("router_turned"), sem("router_ready")
        x_loaded, c_loaded, stored = sem("x_loaded"), sem("c_loaded"), sem("stored")
        bank_filled, bank_rounded, bank_emptied = sem("bank_filled"), sem("bank_rounded"), sem("bank_emptied")
        ln_stats = [sem(f"ln_stats{k + 1}") for k in range(3)]
        ln_moments = [sem(f"ln_moments{k + 1}") for k in range(3)]
        ln_rstd = [sem(f"ln_rstd{k + 1}") for k in range(3)]
        ln_done = [sem(f"ln_done{k + 1}") for k in range(3)]
        relay_in = {n: sem(f"relay_in_{n}") for n in relay}
        relay_out = {n: sem(f"relay_out_{n}") for n in relay}
        self_scored, self_maxed, self_exped = sem("self_scored"), sem("self_maxed"), sem("self_exped")
        self_inverted, self_weighed = sem("self_inverted"), sem("self_weighed")
        w_laid, w_spread, o1_ready = sem("w_laid"), sem("w_spread"), sem("o1_ready")
        k1_laid = sem("k1_laid")
        x_o1_ready, x1_ready, x1_o2_ready, x2_ready = sem("x_o1_ready"), sem("x1_ready"), sem("x1_o2_ready"), sem("x2_ready")
        cross_scored, cross_maxed, cross_exped = sem("cross_scored"), sem("cross_maxed"), sem("cross_exped")
        cross_turned, e2_by_act, e2_by_dve = sem("cross_turned"), sem("e2_by_act"), sem("e2_by_dve")
        cross_attended, cross_inverted, o2_ready = sem("cross_attended"), sem("cross_inverted"), sem("o2_ready")
        logits_ready, r_maxed, r_exped = sem("logits_ready"), sem("r_maxed"), sem("r_exped")
        r_step, routed = sem("r_step"), sem("routed")
        expert_ready, base_ready, first_summed, second_scaled, second_summed = (
            sem("expert_ready"), sem("base_ready"), sem("first_summed"), sem("second_scaled"), sem("second_summed"))

        passed = {e: sem(f"passed_{n}") for n, e in (("sp", nc.sync.engine), ("pool", nc.gpsimd.engine), ("dve", nc.vector.engine))}

        block = stack.enter_context(nc.Block())

        x_g = x.rearrange("(g b) t c -> g t b c", b=PAIR)
        c_g = ctx.rearrange("(g b) t c -> g t b c", b=PAIR)
        out_g = out.rearrange("(g b) t c -> g t b c", b=PAIR)

        def w_source(n):
            if n not in b_dram:
                return [w_raw[n]]
            return [w_raw[n][:, c, :].rearrange("p (l m x) -> p m x l", m=C, x=HD) for c in range(C)]

        def w_out(n, part):
            if n not in b_dram:
                return [W[n][:, part]]
            return [W[n][:, part, c, :].rearrange("p (m x l) -> p m x l", m=C, x=HD) for c in range(C)]

        def pipeline(eng, iteration):
            for i in range(FIRST):
                iteration(i)
            with eng.Fori(FIRST, LAST) as i:
                iteration(i)
            for i in range(LAST, NG + STAGES - 1):
                iteration(i)

        @block.sync
        def _(sp):
            with nc.allow_non_contiguous_dma("biases by channel, once"):
                sp.dma_start(x_in[:], x_g[0]).then_inc(x_loaded, 16)
                for n in names:
                    sp.dma_start(w_raw[n], w_dram[n].rearrange("(c p) n -> p c n", p=P)).then_inc(weights_in, 16)
                for n, b in b_dram.items():
                    for m in range(C):
                        sp.dma_start(bcol_raw[:, B_AT[n], m:m + 1],
                                     b.rearrange("(l m x o) -> m x l o", m=C, x=HD, o=1)[m]).then_inc(bias_in, 16)
                for n, b in (("v1", bv1), ("o1", bo1), ("v2", bv2), ("o2", bo2)):
                    sp.dma_start(brow[:, R_AT[n], :], b.partition_broadcast(P)).then_inc(bias_in, 16)
                sp.dma_start(router_raw[:], router).then_inc(router_in, 16)

            for c in range(C):
                sp.dma_start(e_raw[:, c, :].rearrange("p (e n) -> p e n", n=D),
                             experts[:, c * P:(c + 1) * P, :].rearrange("e p n -> p e n")).then_inc(experts_in, 16)
            sp.wait_ge(zeros_ready, 2)

            def relay_write(g, n, split, done):
                wait_alone(sp, bank_emptied, done)
                wait_alone(sp, relay_out[n], 2 * 16 * g)
                to = relay[n].rearrange("j x (l c) b t -> (x l) j c (b t)", c=C)
                both, high = RELAY_BOTH[n[0]], RELAY_HIGH[n[0]]
                sp.dma_start(to[:, both:both + 2].rearrange("p j c t -> p j (c t)"),
                             split[:].rearrange("p j c t -> p j (c t)").bitcast(F32)).then_inc(relay_in[n], 16)
                sp.dma_start(to[:, high].rearrange("p c t -> p (c t)"),
                             split[:, 0].rearrange("p c t -> p (c t)").bitcast(F32)).then_inc(relay_in[n], 16)

            def relay_read(g, n, target, scored, count=UNITS):
                wait_alone(sp, relay_in[n], 2 * 16 * (g + 1))
                wait_alone(sp, scored, count * g)
                for b in range(PAIR):
                    rows = target[b * ROWS:(b + 1) * ROWS]
                    sp.dma_start((rows[:, b] if len(target.shape) == 4 else rows).bitcast(F32),
                                 relay[n][:, :, :, b, :].rearrange("j x g t -> (j x) g t")).then_inc(relay_out[n], 16)

            def iteration(i):
                gp, gs, gc, ge = i - PROJECT, i - SELF, i - CROSS, i - EXPERTS

                def write_k2():
                    if active(i, CROSS):
                        relay_write(gc, "k2", k_split, order(i, "k2") + 1)

                def write_q2():
                    if active(i, CROSS):
                        relay_write(gc, "q2", q_split, order(i, "q2") + 1)

                def write_q1():
                    if active(i, PROJECT):
                        relay_write(gp, "q1", q_split, order(i, "q1") + 1)

                def write_k1():
                    if active(i, PROJECT):
                        relay_write(gp, "k1", k_split, order(i, "k1") + 1)

                def read_k2():
                    if active(i, CROSS):
                        relay_read(gc, "k2", ks2, cross_scored)

                def read_q2():
                    if active(i, CROSS):
                        relay_read(gc, "q2", qs2, cross_scored)

                def read_q1():
                    if active(i, PROJECT):
                        relay_read(gp, "q1", qs1, self_scored)

                def read_k1():
                    if active(i, PROJECT):
                        relay_read(gp, "k1", ks1_in, k1_laid, 1)

                def load_context():
                    if active(i, SELF):
                        if active(i, CROSS):
                            wait_alone(sp, bank_filled, order(i, "turn_ctx") + 1)
                        sp.dma_start(c_in[:], c_g[gs]).then_inc(c_loaded, 16)

                def load_x():
                    if active(i + 1, PROJECT):
                        wait_alone(sp, ln_done[0], gp + 1)
                        wait_alone(sp, x_o1_ready, gp + 1)
                        sp.dma_start(x_in[:], x_g[gp + 1]).then_inc(x_loaded, 16)

                def spread_w():
                    if active(i, SELF):
                        wait_alone(sp, w_laid, gs + 1)
                        wait_alone(sp, o1_ready, gs)
                        for b in range(PAIR):
                            sp.dma_start(w_tok[:, b, :], w_row[b * HEADS:(b + 1) * HEADS]).then_inc(w_spread, 16)

                def store():
                    if active(i, EXPERTS):
                        wait_alone(sp, first_summed, EX * (ge + 1))
                        wait_alone(sp, second_summed, EX * (ge + 1))
                        sp.dma_start(out_g[ge], y).then_inc(stored, 16)

                load_context()
                write_k2()
                write_q2()
                read_k2()
                read_q2()
                write_k1()
                spread_w()
                write_q1()
                read_k1()
                read_q1()
                load_x()
                store()

            for i in range(FIRST):
                iteration(i)
            with sp.Fori(FIRST, LAST - 1) as i:
                iteration(i)
            for i in range(LAST - 1, NG + STAGES - 1):
                iteration(i)
            sp.wait_ge(stored, 16 * NG)

        @block.gpsimd
        def _(pool):
            for m in (ident, ident_bf, mask_bf):
                nc.gpsimd.memset(m[:], 0.0).then_inc(ident_zero, 1)
            pool.wait_ge(ident_zero, 3)
            for m in (ident, ident_bf):
                nc.gpsimd.affine_select(out=m[:], in_=m[:], compare_op=ALU.not_equal, fill=1.0, base=0,
                                        pattern=[[-1, P]], channel_multiplier=1).then_inc(ident_ready, 1)
            nc.gpsimd.affine_select(out=mask_bf[:], in_=mask_bf[:], compare_op=ALU.is_ge, fill=MASKED,
                                    base=WINDOW // 2, pattern=[[-1, P]], channel_multiplier=1).then_inc(mask_ready, 1)
            pool.wait_ge(mask_ready, 1)
            nc.gpsimd.affine_select(out=mask_bf[:], in_=mask_bf[:], compare_op=ALU.is_ge, fill=MASKED,
                                    base=WINDOW // 2, pattern=[[1, P]], channel_multiplier=-1).then_inc(mask_ready, 1)
            for s in (qs1[:].bitcast(F32), ks2[:].bitcast(F32), rsum1[:]):
                nc.gpsimd.memset(s, 0.0).then_inc(zeros_ready, 1)
            for e in range(EX):
                nc.gpsimd.memset(falling[:, :, e:e + 1], float(EX - e)).then_inc(falling_ready, 1)
            nc.gpsimd.memset(minus_half[:], -0.5).then_inc(falling_ready, 1)
            pool.wait_ge(falling_ready, EX + 1)
            pool.wait_ge(bias_in, (4 + 4 * C) * 16)

            def invert_deviation(k, g):
                wait_alone(pool, ln_moments[k], g + 1)
                nc.gpsimd.tensor_scalar(rstd[k][:], moments[k][:, :, 1], EPS, None, ALU.add).then_inc(ln_rstd[k], 1)
                pool.wait_ge(ln_rstd[k], 2 * g + 1)
                nc.gpsimd.tensor_tensor(rstd[k][:], rstd[k][:], minus_half[:], ALU.pow).then_inc(ln_rstd[k], 1)

            def add_bias(to, source, n):
                return nc.gpsimd.tensor_tensor(
                    to[:], source[:], brow[:, R_AT[n], :].unsqueeze(1).to_broadcast([P, PAIR, D]), ALU.add)

            def iteration(i):
                gp, gs, gc, ge = i - PROJECT, i - SELF, i - CROSS, i - EXPERTS

                def deviation3():
                    if active(i, EXPERTS):
                        invert_deviation(2, ge)

                def deviation1():
                    if active(i, PROJECT):
                        invert_deviation(0, gp)

                def deviation2():
                    if active(i, SELF):
                        invert_deviation(1, gs)

                def residual2():
                    if active(i, CROSS):
                        pool.wait_ge(x1_ready, gc + 1)
                        wait(pool, x2_ready, gc)
                        add_bias(x1_o2, x1, "o2").then_inc(x1_o2_ready, 1)

                def residual1():
                    if active(i, PROJECT):
                        pool.wait_ge(x_loaded, 16 * (gp + 1))
                        wait(pool, x1_ready, gp)
                        add_bias(x_o1, x_in, "o1").then_inc(x_o1_ready, 1)

                def sum_second():
                    if not active(i, EXPERTS):
                        return
                    for e in range(EX):
                        pool.wait_ge(second_scaled, EX * ge + e + 1)
                        if e:
                            pool.wait_ge(second_summed, EX * ge + e)
                        nc.gpsimd.tensor_tensor(y[:, 1, :], y[:, 1, :], scaled[:, e % 4, :] if e else x2[:, 1, :], ALU.add)\
                            .then_inc(second_summed, 1)

                def weigh_v():
                    if active(i, SELF):
                        pool.wait_ge(w_spread, 2 * 16 * (gs + 1))
                        if active(i - 1, SELF) and not (isinstance(i, int) and gs == 0):
                            pool.wait_ge(bank_filled, order(i - 1, "turn_o1") + 1)
                        nc.gpsimd.tensor_tensor(
                            o1[:].rearrange("p b (g x) -> p (b g) x", x=HD),
                            v1[:].rearrange("p b (g x) -> p (b g) x", x=HD),
                            w_tok[:].rearrange("p b g -> p (b g)").unsqueeze(2).to_broadcast([P, PAIR * HEADS, HD]),
                            ALU.mult).then_inc(o1_ready, 1)

                deviation1()
                deviation3()
                sum_second()
                weigh_v()
                residual2()
                deviation2()
                residual1()

            pipeline(pool, iteration)

        @block.scalar
        def _(act):
            act.wait_ge(weights_in, 8 * 16)
            for n in names:
                for to, source in zip(w_out(n, 0), w_source(n)):
                    last = nc.scalar.activation(to, source, ACT.Copy, scale=w_scale[n])
                last.then_inc(w_high, 1)
            act.wait_ge(bcol_ready, 4)

            def high(i, name, target):
                act.wait_ge(bank_filled, order(i, name) + 1)
                nc.scalar.activation(target[:, 0].rearrange("p c t -> p (c t)"), bank[:, bank_of(name), :], ACT.Copy)\
                    .then_inc(bank_rounded, 1)

            def high_biased(i, name, target):
                act.wait_ge(bank_filled, order(i, name) + 1)
                for c in range(C):
                    last = nc.scalar.activation(target[:, 0, c, :], bank[:, bank_of(name), c * TOK2:(c + 1) * TOK2],
                                                ACT.Identity, bias=bcol[:, B_AT[name], c:c + 1])
                last.then_inc(bank_rounded, 1)

            def exps(maxed, exped, g, u, nmax, e, total):
                act.wait_ge(maxed, UNITS * g + u + 1)
                for hh in range(2):
                    for b in range(PAIR):
                        col = (hh * PAIR + b) * P
                        last = nc.scalar.activation(e[:, u % SLOTS, hh, b, :], scores[:, u % 2, col:col + P], ACT.Exp,
                                                    bias=nmax[:, u, hh * PAIR + b:hh * PAIR + b + 1],
                                                    accum_out=total[:, b, 2 * u + hh:2 * u + hh + 1])
                last.then_inc(exped, 1)

            def iteration(i):
                gp, gs, gc, ge = i - PROJECT, i - SELF, i - CROSS, i - EXPERTS

                def split_experts():
                    if isinstance(i, int) and i == SPLIT_AT:
                        act.wait_ge(experts_in, C * 16)
                        for c in range(C):
                            nc.scalar.activation(WE[:, 0, c, :], e_raw[:, c, :], ACT.Copy).then_inc(w_high, 1)

                def self_exps(u):
                    if active(i, SELF):
                        if isinstance(i, int) and i == SELF and u == 0:
                            act.wait_ge(w_low, 8)
                        wait(act, self_weighed, UNITS * gs + u + 1 - SLOTS)
                        exps(self_maxed, self_exped, gs, u, nmax1, e1, sum1)

                def cross_exps(u):
                    if active(i, CROSS):
                        if isinstance(i, int) and i == CROSS and u == 0:
                            act.wait_ge(w_low, 8 + C)
                        wait(act, cross_turned, UNITS * gc + u + 1 - SLOTS)
                        exps(cross_maxed, cross_exped, gc, u, nmax2, e2, sum2)

                def copy_turned(u):
                    if active(i, CROSS):
                        act.wait_ge(cross_turned, UNITS * gc + u + 1)
                        wait(act, cross_attended, UNITS * gc + u - 1)
                        nc.scalar.activation(e2_t[:, 0].rearrange("p h b a -> p (h b a)"), turned_e[:], ACT.Copy)\
                            .then_inc(e2_by_act, 1)

                def scale_second(q):
                    if not active(i, EXPERTS):
                        return
                    act.wait_ge(expert_ready, FUNITS * ge + 2 * q + 2)
                    if q == 0:
                        act.wait_ge(routed, ge + 1)
                        wait(act, stored, 16 * ge)
                    for e in (2 * q, 2 * q + 1):
                        source = attended[:, (e % 2) * D:(e % 2 + 1) * D]
                        if e == 0:
                            ins = nc.scalar.activation(y[:, 1, :], source, ACT.Identity,
                                                       bias=r_bias[:, 1:2], scale=r_c[:, 1, 0:1])
                        else:
                            wait(act, second_summed, EX * ge + (e - 3 if e > 4 else 0))
                            ins = nc.scalar.activation(scaled[:, e % 4, :], source, ACT.Copy, scale=r_c[:, 1, e:e + 1])
                        ins.then_inc(second_scaled, 1)

                def first_base():
                    if active(i, EXPERTS):
                        act.wait_ge(routed, ge + 1)
                        wait(act, stored, 16 * ge)
                        nc.scalar.activation(y[:, 0, :], x2[:, 0, :], ACT.Identity, bias=r_bias[:, 0:1])\
                            .then_inc(base_ready, 1)

                def router_exps():
                    if active(i, EXPERTS):
                        act.wait_ge(r_maxed, ge + 1)
                        for b in range(PAIR):
                            last = nc.scalar.activation(r_exp[:, b, :], logits[:, b, :], ACT.Exp, bias=r_nmax[:, b:b + 1],
                                                        accum_out=r_sum[:, b:b + 1])
                        last.then_inc(r_exped, 1)

                def high_o2():
                    if active(i, EXPERTS):
                        high(i, "turn_o2", turned_o)

                def high_ctx():
                    if active(i, CROSS):
                        high(i, "turn_ctx", turned_in)

                def high_h2():
                    if active(i, CROSS):
                        high(i, "turn_h2", turned_h)

                def high_k2():
                    if active(i, CROSS):
                        wait(act, relay_in["k1"], 2 * 16 * (min(i, NG) if isinstance(i, int) else i))
                        high_biased(i, "k2", k_split)

                def high_q2():
                    if active(i, CROSS):
                        wait(act, relay_in["q1"], 2 * 16 * (min(i, NG) if isinstance(i, int) else i))
                        high_biased(i, "q2", q_split)

                def high_h3():
                    if active(i, EXPERTS):
                        high(i, "turn_h3", turned_h)

                def high_h1():
                    if active(i, PROJECT):
                        high(i, "turn_h1", turned_in)

                def high_q1():
                    if active(i, PROJECT):
                        if active(i, CROSS):
                            act.wait_ge(relay_in["q2"], 2 * 16 * (gc + 1))
                        else:
                            wait(act, relay_in["q1"], 2 * 16 * gp)
                        high_biased(i, "q1", q_split)

                def high_k1():
                    if active(i, PROJECT):
                        if active(i, CROSS):
                            act.wait_ge(relay_in["k2"], 2 * 16 * (gc + 1))
                        else:
                            wait(act, relay_in["k1"], 2 * 16 * gp)
                        high_biased(i, "k1", k_split)

                def high_o1():
                    if active(i, SELF):
                        high(i, "turn_o1", turned_o)

                high_ctx()
                high_o2()
                high_h2()
                self_exps(0)
                high_k2()
                self_exps(1)
                self_exps(2)
                high_q2()
                self_exps(3)
                high_h3()
                self_exps(4)
                high_h1()
                self_exps(5)
                router_exps()
                self_exps(6)
                self_exps(7)
                scale_second(0)
                first_base()
                high_k1()
                split_experts()
                high_q1()
                cross_exps(0)
                cross_exps(1)
                scale_second(1)
                scale_second(2)
                cross_exps(2)
                cross_exps(3)
                copy_turned(0)
                scale_second(3)
                cross_exps(4)
                copy_turned(2)
                cross_exps(5)
                cross_exps(6)
                copy_turned(4)
                high_o1()
                cross_exps(7)
                copy_turned(6)

            pipeline(act, iteration)

        @block.vector
        def _(dve):
            dve.wait_ge(bias_in, (4 + 4 * C) * 16)
            for n in b_dram:
                nc.vector.tensor_scalar(bcol[:, B_AT[n], :], bcol_raw[:, B_AT[n], :], w_scale[n], None, ALU.mult)\
                    .then_inc(bcol_ready, 1)
            dve.wait_ge(bcol_ready, 4)
            for k, n in enumerate(names):
                dve.wait_ge(w_high, k + 1)
                for to, source, high_part in zip(w_out(n, 1), w_source(n), w_out(n, 0)):
                    last = nc.vector.scalar_tensor_tensor(out=to, in0=source, scalar=w_scale[n], in1=high_part,
                                                          op0=ALU.mult, op1=ALU.subtract)
                last.then_inc(w_low, 1)
            dve.wait_ge(router_turned, 1)
            nc.vector.tensor_copy(router_t[:], router_ps).then_inc(router_ready, 1)
            dve.wait_ge(falling_ready, EX)
            dve.wait_ge(zeros_ready, 3)

            def low(i, name, target):
                dve.wait_ge(bank_rounded, order(i, name, rounded=True) + 1)
                nc.vector.tensor_tensor(target[:, 1].rearrange("p c t -> p (c t)"), bank[:, bank_of(name), :],
                                        target[:, 0].rearrange("p c t -> p (c t)"), ALU.subtract)\
                    .then_inc(bank_emptied, 1)

            def low_biased(i, name, target):
                dve.wait_ge(bank_rounded, order(i, name, rounded=True) + 1)
                for c in range(C):
                    last = nc.vector.scalar_tensor_tensor(
                        out=target[:, 1, c, :], in0=bank[:, bank_of(name), c * TOK2:(c + 1) * TOK2],
                        scalar=bcol[:, B_AT[name], c:c + 1], in1=target[:, 0, c, :], op0=ALU.add, op1=ALU.subtract)
                last.then_inc(bank_emptied, 1)

            def statistics(k, g, source, ready):
                for b in range(PAIR):
                    last = nc.vector.bn_stats(stats[k][:, b, :], source[:, b, :])
                last.then_inc(ready, 1)
                wait_alone(dve, ready, g + 1)
                for b in range(PAIR):
                    last = nc.vector.bn_aggr(moments[k][:, b, :], stats[k][:, b, :])
                last.then_inc(ln_moments[k], 1)

            def normalize(k, g, source):
                dve.wait_ge(ln_rstd[k], 2 * g + 2)
                for b in range(PAIR):
                    last = nc.vector.tensor_scalar(h[k][:, b, :], source[:, b, :], moments[k][:, b, 0:1],
                                                   rstd[k][:, b:b + 1], ALU.subtract, ALU.mult)
                last.then_inc(ln_done[k], 1)

            def maxima(scored, maxed, g, u, nmax):
                dve.wait_ge(scored, UNITS * g + u + 1)
                nc.vector.tensor_reduce(nmax[:, u, :], scores[:, u % 2, :].rearrange("p (s a) -> p s a", a=P), AX.X,
                                        ALU.max, negate=True).then_inc(maxed, 1)

            def in_bank(name):
                return bank[:, bank_of(name), :].rearrange("p (b n) -> p b n", b=PAIR)

            def with_bias(i, name, to, done):
                dve.wait_ge(bank_filled, order(i, name) + 1)
                wait(dve, *done)
                nc.vector.tensor_tensor(to[:], in_bank(name),
                                        brow[:, R_AT[name], :].unsqueeze(1).to_broadcast([P, PAIR, D]), ALU.add)\
                    .then_inc(bank_emptied, 1)

            def iteration(i):
                gp, gs, gc, ge = i - PROJECT, i - SELF, i - CROSS, i - EXPERTS

                def split_experts():
                    if isinstance(i, int) and i == SPLIT_AT:
                        for c in range(C):
                            dve.wait_ge(w_high, 8 + c + 1)
                            nc.vector.tensor_tensor(WE[:, 1, c, :], e_raw[:, c, :], WE[:, 0, c, :], ALU.subtract)\
                                .then_inc(w_low, 1)

                def self_max(u):
                    if active(i, SELF):
                        maxima(self_scored, self_maxed, gs, u, nmax1)

                def self_invert(u):
                    if active(i, SELF):
                        dve.wait_ge(self_exped, UNITS * gs + u + 1)
                        nc.vector.reciprocal(rsum1_places[:, :, 2 * u:2 * u + 2], sum1[:, :, 2 * u:2 * u + 2])\
                            .then_inc(self_inverted, 1)

                def cross_max(u):
                    if active(i, CROSS):
                        maxima(cross_scored, cross_maxed, gc, u, nmax2)

                def copy_turned(u):
                    if active(i, CROSS):
                        dve.wait_ge(cross_turned, UNITS * gc + u + 1)
                        wait(dve, cross_attended, UNITS * gc + u - 1)
                        nc.vector.tensor_copy(e2_t[:, 1].rearrange("p h b a -> p (h b a)"), turned_e[:])\
                            .then_inc(e2_by_dve, 1)

                def sum_first(q):
                    if not active(i, EXPERTS):
                        return
                    dve.wait_ge(expert_ready, FUNITS * ge + 2 * q + 1)
                    for e in (2 * q, 2 * q + 1):
                        if e == 0:
                            dve.wait_ge(base_ready, ge + 1)
                        else:
                            dve.wait_ge(first_summed, EX * ge + e)
                        nc.vector.scalar_tensor_tensor(
                            out=y[:, 0, :], in0=turned_e[:, (e % 2) * D:(e % 2 + 1) * D], scalar=r_c[:, 0, e:e + 1],
                            in1=y[:, 0, :], op0=ALU.mult, op1=ALU.add).then_inc(first_summed, 1)

                STEPS = 18
                done = [0]

                def step(ins):
                    done[0] += 1
                    ins.then_inc(r_step, 1)
                    dve.wait_ge(r_step, STEPS * ge + done[0])

                def wide(a, n):
                    return a.unsqueeze(2).to_broadcast([P, PAIR, n])

                def router_max():
                    if active(i, EXPERTS):
                        dve.wait_ge(logits_ready, ge + 1)
                        nc.vector.tensor_reduce(r_nmax[:], logits, AX.X, ALU.max, negate=True).then_inc(r_maxed, 1)

                def route():
                    if not active(i, EXPERTS):
                        return
                    dve.wait_ge(r_exped, ge + 1)
                    step(nc.vector.reciprocal(r_rsum[:], r_sum[:]))
                    step(nc.vector.tensor_tensor(r_p[:], r_exp[:], wide(r_rsum[:], EX), ALU.mult))
                    p = r_p
                    for j in range(2):
                        step(nc.vector.tensor_reduce(r_top[:, :, j], p[:], AX.X, ALU.max))
                        step(nc.vector.tensor_tensor(r_eq[:], p[:], wide(r_top[:, :, j], EX), ALU.is_equal))
                        step(nc.vector.tensor_tensor(r_key[:], r_eq[:], falling[:], ALU.mult))
                        step(nc.vector.tensor_reduce(r_first[:], r_key[:], AX.X, ALU.max))
                        step(nc.vector.tensor_tensor(r_hot[j][:], falling[:], wide(r_first[:], EX), ALU.is_equal))
                        if j == 0:
                            step(nc.vector.scalar_tensor_tensor(out=r_rest[:], in0=r_hot[0][:], scalar=-2.0, in1=r_p[:],
                                                                op0=ALU.mult, op1=ALU.add))
                            p = r_rest
                    step(nc.vector.scalar_tensor_tensor(out=r_norm[:], in0=r_top[:, :, 0], scalar=TOP_EPS,
                                                        in1=r_top[:, :, 1], op0=ALU.add, op1=ALU.add))
                    step(nc.vector.reciprocal(r_rnorm[:], r_norm[:]))
                    step(nc.vector.tensor_tensor(r_w[:], r_top[:], wide(r_rnorm[:], 2), ALU.mult))
                    nc.vector.tensor_tensor(r_wh[0][:], r_hot[0][:], wide(r_w[:, :, 0], EX), ALU.mult)
                    nc.vector.tensor_tensor(r_wh[1][:], r_hot[1][:], wide(r_w[:, :, 1], EX), ALU.mult)
                    step(nc.vector.tensor_tensor(r_pw[:], r_top[:], r_w[:], ALU.mult))
                    nc.vector.tensor_reduce(r_bias[:], r_pw[:], AX.X, ALU.add)
                    step(nc.vector.tensor_tensor(r_c[:], r_wh[0][:], r_wh[1][:], ALU.add))
                    assert done[0] == STEPS, done
                    nc.vector.tensor_copy(r_key[:, :, 0:1], r_c[:, :, 0:1]).then_inc(routed, 1)

                def low_o2():
                    if active(i, EXPERTS):
                        low(i, "turn_o2", turned_o)

                def low_ctx():
                    if active(i, CROSS):
                        low(i, "turn_ctx", turned_in)

                def low_h2():
                    if active(i, CROSS):
                        low(i, "turn_h2", turned_h)

                def add_x2():
                    if active(i, EXPERTS):
                        dve.wait_ge(bank_filled, order(i, "out2") + 1)
                        dve.wait_ge(x1_o2_ready, ge + 1)
                        wait(dve, second_summed, EX * ge)
                        nc.vector.tensor_tensor(x2[:], in_bank("out2"), x1_o2[:], ALU.add).then_inc(bank_emptied, 1)
                        dve.wait_ge(bank_emptied, order(i, "out2") + 1)
                        statistics(2, ge, x2, x2_ready)

                def normalize3():
                    if active(i, EXPERTS):
                        normalize(2, ge, x2)

                def low_k2():
                    if active(i, CROSS):
                        low_biased(i, "k2", k_split)

                def low_q2():
                    if active(i, CROSS):
                        low_biased(i, "q2", q_split)

                def add_v2():
                    if active(i, CROSS):
                        with_bias(i, "v2", v2, (cross_attended, UNITS * gc))

                def low_h3():
                    if active(i, EXPERTS):
                        low(i, "turn_h3", turned_h)

                def statistics1():
                    if active(i, PROJECT):
                        dve.wait_ge(x_loaded, 16 * (gp + 1))
                        statistics(0, gp, x_in, ln_stats[0])

                def normalize1():
                    if active(i, PROJECT):
                        if active(i - 1, PROJECT):
                            dve.wait_ge(bank_filled, order(i - 1, "turn_h1") + 1)
                        normalize(0, gp, x_in)

                def copy_w_row():
                    if active(i, SELF):
                        dve.wait_ge(self_weighed, UNITS * (gs + 1))
                        wait(dve, w_spread, 2 * 16 * gs)
                        nc.vector.tensor_copy(w_row[:], w_sum.rearrange("p (g t) -> p t g", t=8)).then_inc(w_laid, 1)

                def low_h1():
                    if active(i, PROJECT):
                        low(i, "turn_h1", turned_in)

                def low_q1():
                    if active(i, PROJECT):
                        low_biased(i, "q1", q_split)

                def low_k1():
                    if active(i, PROJECT):
                        low_biased(i, "k1", k_split)

                def low_o1():
                    if active(i, SELF):
                        low(i, "turn_o1", turned_o)

                def add_v1():
                    if active(i, PROJECT):
                        with_bias(i, "v1", v1, (o1_ready, gp))

                def add_x1():
                    if active(i, SELF):
                        dve.wait_ge(bank_filled, order(i, "out1") + 1)
                        dve.wait_ge(x_o1_ready, gs + 1)
                        wait(dve, x1_o2_ready, gs)
                        nc.vector.tensor_tensor(x1[:], in_bank("out1"), x_o1[:], ALU.add).then_inc(bank_emptied, 1)
                        dve.wait_ge(bank_emptied, order(i, "out1") + 1)
                        statistics(1, gs, x1, x1_ready)

                def normalize2():
                    if active(i, SELF):
                        if active(i, CROSS):
                            dve.wait_ge(bank_filled, order(i, "turn_h2") + 1)
                        normalize(1, gs, x1)

                def divide_o2():
                    if active(i, CROSS):
                        dve.wait_ge(cross_exped, UNITS * (gc + 1))
                        nc.vector.reciprocal(rsum2[:], sum2[:]).then_inc(cross_inverted, 1)
                        dve.wait_ge(cross_inverted, gc + 1)
                        dve.wait_ge(cross_attended, UNITS * (gc + 1))
                        if active(i, EXPERTS):
                            dve.wait_ge(bank_filled, order(i, "turn_o2") + 1)
                        nc.vector.tensor_tensor(
                            o2[:].rearrange("p b (g x) -> p (b g) x", x=HD),
                            attended[:].rearrange("p (s x) -> p s x", x=HD),
                            rsum2[:].rearrange("p b g -> p (b g)").unsqueeze(2).to_broadcast([P, PAIR * HEADS, HD]),
                            ALU.mult).then_inc(o2_ready, 1)

                def lay_k1():
                    if active(i, PROJECT):
                        dve.wait_ge(relay_out["k1"], 2 * 16 * (gp + 1))
                        wait(dve, self_scored, UNITS * gp)
                        nc.vector.tensor_copy(ks1[:].rearrange("r e (g t) -> r e g t", t=8),
                                              ks1_in[:].rearrange("r g (e t) -> r e g t", t=8)).then_inc(k1_laid, 1)

                low_ctx()
                self_max(0)
                self_max(1)
                low_o2()
                statistics1()
                self_invert(0)
                low_h2()
                low_k2()
                self_max(2)
                self_invert(1)
                add_x2()
                self_max(3)
                self_invert(2)
                low_q2()
                normalize3()
                normalize1()
                self_invert(3)
                self_max(4)
                add_v2()
                low_h3()
                self_max(5)
                self_max(6)
                router_max()
                self_invert(4)
                low_h1()
                self_max(7)
                route()
                sum_first(0)
                cross_max(0)
                self_invert(5)
                cross_max(1)
                sum_first(1)
                low_k1()
                split_experts()
                cross_max(2)
                sum_first(2)
                self_invert(6)
                cross_max(3)
                low_q1()
                sum_first(3)
                self_invert(7)
                cross_max(4)
                copy_w_row()
                copy_turned(1)
                cross_max(5)
                cross_max(6)
                copy_turned(3)
                cross_max(7)
                add_v1()
                low_o1()
                copy_turned(5)
                lay_k1()
                add_x1()
                copy_turned(7)
                divide_o2()
                normalize2()

            pipeline(dve, iteration)

        @block.tensor
        def _(pe):
            pe.wait_ge(ident_ready, 2)
            pe.wait_ge(router_in, 16)
            for c in range(C):
                last = nc.tensor.transpose(router_ps[:, c, :], router_raw[:, c * P:(c + 1) * P], ident[0:EX, 0:EX])
            last.then_inc(router_turned, 1)
            pe.wait_ge(router_ready, 1)
            pe.wait_ge(w_low, 8)
            pe.wait_ge(mask_ready, 2)

            PRODUCTS = ((0, 0), (0, 1), (1, 0))

            def turn(i, name, source):
                wait(pe, bank_emptied, emptied_before(i, name))
                for c in range(C):
                    for b in range(PAIR):
                        last = nc.tensor.transpose(bank[:, bank_of(name), (c * PAIR + b) * P:(c * PAIR + b + 1) * P],
                                                   source[:, b, c * P:(c + 1) * P], ident[:])
                last.then_inc(bank_filled, 1)

            def project_turned(i, name, weights, turned):
                wait(pe, bank_emptied, emptied_before(i, name))
                for m in range(C):
                    for k, (wp, xp) in enumerate(PRODUCTS):
                        for c in range(C):
                            last = nc.tensor.matmul(
                                bank[:, bank_of(name), m * TOK2:(m + 1) * TOK2], weights[:, wp, c, m * P:(m + 1) * P],
                                turned[:, xp, c, :], start=(k == 0 and c == 0), stop=(k == 2 and c == C - 1))
                last.then_inc(bank_filled, 1)

            def project(i, name, weights, turned):
                wait(pe, bank_emptied, emptied_before(i, name))
                for b in range(PAIR):
                    for k, (wp, xp) in enumerate(PRODUCTS):
                        for c in range(C):
                            last = nc.tensor.matmul(
                                bank[:, bank_of(name), b * D:(b + 1) * D], turned[:, xp, c, b * TOK:(b + 1) * TOK],
                                weights[:, wp, c, :], start=(k == 0 and c == 0), stop=(k == 2 and c == C - 1))
                last.then_inc(bank_filled, 1)

            def iteration(i):
                gp, gs, gc, ge = i - PROJECT, i - SELF, i - CROSS, i - EXPERTS

                def self_scores(u):
                    if not active(i, SELF):
                        return
                    if u == 0:
                        pe.wait_ge(relay_out["q1"], 2 * 16 * (gs + 1))
                        pe.wait_ge(k1_laid, gs + 1)
                    wait(pe, self_exped, UNITS * gs + u - 1)
                    if u < 2:
                        wait(pe, cross_exped, UNITS * (gs - 1))
                    for hh in range(2):
                        e = 2 * u + hh
                        t = 8 * e
                        last = nc.tensor.matmul(scores[:, u % 2, hh * TOK2:(hh + 1) * TOK2],
                                                ks1[:, e, :], qs1[:, :, :, t:t + 8], start=True, stop=True)
                    last.then_inc(self_scored, 1)

                def self_weights(u):
                    if not active(i, SELF):
                        return
                    pe.wait_ge(self_inverted, UNITS * gs + u + 1)
                    if u == 0:
                        wait(pe, w_laid, gs)
                    for hh in range(2):
                        for b in range(PAIR):
                            e = 2 * u + hh
                            row = b * HEADS + e
                            last = nc.tensor.matmul(w_sum, rsum1[:, PAIR * HEADS * row:PAIR * HEADS * (row + 1)],
                                                    e1[:, u % SLOTS, hh, b, :], start=(u == 0 and hh == 0 and b == 0),
                                                    stop=(u == UNITS - 1 and hh == 1 and b == PAIR - 1))
                    last.then_inc(self_weighed, 1)

                def cross_scores(u):
                    if not active(i, CROSS):
                        return
                    if u == 0:
                        pe.wait_ge(relay_out["q2"], 2 * 16 * (gc + 1))
                        pe.wait_ge(relay_out["k2"], 2 * 16 * (gc + 1))
                    wait(pe, cross_exped, UNITS * gc + u - 1)
                    if u < 2:
                        wait(pe, self_exped, UNITS * (min(gc + 2, NG) if isinstance(i, int) else gc + 2))
                    nc.tensor.matmul(scores[:, u % 2, :], ident_bf[:], mask_bf[:].unsqueeze(1).to_broadcast([P, 4, P]),
                                     start=True, stop=False, skip_group_check=True)
                    for hh in range(2):
                        e = 2 * u + hh
                        last = nc.tensor.matmul(scores[:, u % 2, hh * TOK2:(hh + 1) * TOK2], qs2[:, e, :],
                                                ks2[:, :, e, :], start=False, stop=True, skip_group_check=True)
                    last.then_inc(cross_scored, 1)

                def cross_turn(u):
                    if not active(i, CROSS):
                        return
                    pe.wait_ge(cross_exped, UNITS * gc + u + 1)
                    if u == 0:
                        wait(pe, first_summed, EX * gc)
                        wait(pe, e2_by_dve, UNITS // 2 * gc)
                    elif u % 2:
                        pe.wait_ge(e2_by_act, UNITS // 2 * gc + u // 2 + 1)
                    else:
                        pe.wait_ge(e2_by_dve, UNITS // 2 * gc + u // 2)
                    for hh in range(2):
                        for b in range(PAIR):
                            col = (hh * PAIR + b) * P
                            last = nc.tensor.transpose(turned_e[:, col:col + P], e2[:, u % SLOTS, hh, b, :], ident[:])
                    last.then_inc(cross_turned, 1)

                def cross_attend(u):
                    if not active(i, CROSS):
                        return
                    if u == 0:
                        pe.wait_ge(bank_emptied, order(i, "v2") + 1)
                        wait(pe, second_scaled, EX * gc)
                    pe.wait_ge(*((e2_by_dve, UNITS // 2 * gc + u // 2 + 1) if u % 2 else
                                 (e2_by_act, UNITS // 2 * gc + u // 2 + 1)))
                    for hh in range(2):
                        for b in range(PAIR):
                            e = 2 * u + hh
                            at = (b * HEADS + e) * HD
                            last = nc.tensor.matmul(attended[:, at:at + HD], e2_t[:, u % 2, hh, b, :],
                                                    v2[:, b, e * HD:(e + 1) * HD], start=True, stop=True)
                    last.then_inc(cross_attended, 1)

                def route():
                    if not active(i, EXPERTS):
                        return
                    pe.wait_ge(bank_emptied, order(i, "turn_h3") + 1)
                    wait(pe, r_exped, ge)
                    for b in range(PAIR):
                        for k in range(2 * C):
                            last = nc.tensor.matmul(logits[:, b, :],
                                                    turned_h[:, k // C, k % C, b * TOK:(b + 1) * TOK].bitcast(F32),
                                                    router_t[:, k % C, :], start=(k == 0), stop=(k == 2 * C - 1))
                    last.then_inc(logits_ready, 1)

                def expert_pair(f):
                    if not active(i, EXPERTS):
                        return
                    if f >= PAIR:
                        pe.wait_ge((first_summed, second_scaled)[f % 2], EX * ge + 2 * (f // 2))
                    elif f == 0:
                        if isinstance(i, int) and i == EXPERTS:
                            pe.wait_ge(w_low, 8 + C)
                        pe.wait_ge(e2_by_dve, UNITS // 2 * (ge + 1))
                    else:
                        pe.wait_ge(r_exped, ge + 1)
                    b, col = f % PAIR, (f // PAIR) * 2 * D
                    for k, (wp, xp) in enumerate(PRODUCTS):
                        for c in range(C):
                            last = nc.tensor.matmul((turned_e, attended)[f % 2][:],
                                                    turned_h[:, xp, c, b * TOK:(b + 1) * TOK], WE[:, wp, c, col:col + 2 * D],
                                                    start=(k == 0 and c == 0), stop=(k == 2 and c == C - 1))
                    last.then_inc(expert_ready, 1)

                def turn_o2():
                    if active(i, EXPERTS):
                        pe.wait_ge(o2_ready, ge + 1)
                        turn(i, "turn_o2", o2)

                def turn_ctx():
                    if active(i, CROSS):
                        pe.wait_ge(c_loaded, 16 * (gc + 1))
                        turn(i, "turn_ctx", c_in)

                def turn_h2():
                    if active(i, CROSS):
                        pe.wait_ge(ln_done[1], gc + 1)
                        turn(i, "turn_h2", h[1])

                def turn_h3():
                    if active(i, EXPERTS):
                        pe.wait_ge(ln_done[2], ge + 1)
                        turn(i, "turn_h3", h[2])

                def turn_h1():
                    if active(i, PROJECT):
                        pe.wait_ge(ln_done[0], gp + 1)
                        turn(i, "turn_h1", h[0])

                def turn_o1():
                    if active(i, SELF):
                        pe.wait_ge(o1_ready, gs + 1)
                        turn(i, "turn_o1", o1)

                def project_out2():
                    if active(i, EXPERTS):
                        pe.wait_ge(bank_emptied, order(i, "turn_o2") + 1)
                        project(i, "out2", W["o2"], turned_o)

                def project_k2():
                    if active(i, CROSS):
                        pe.wait_ge(bank_emptied, order(i, "turn_ctx") + 1)
                        project_turned(i, "k2", W["k2"], turned_in)

                def project_v2():
                    if active(i, CROSS):
                        pe.wait_ge(bank_emptied, order(i, "turn_ctx") + 1)
                        project(i, "v2", W["v2"], turned_in)

                def project_q2():
                    if active(i, CROSS):
                        pe.wait_ge(bank_emptied, order(i, "turn_h2") + 1)
                        project_turned(i, "q2", W["q2"], turned_h)

                def project_q1():
                    if active(i, PROJECT):
                        pe.wait_ge(bank_emptied, order(i, "turn_h1") + 1)
                        project_turned(i, "q1", W["q1"], turned_in)

                def project_k1():
                    if active(i, PROJECT):
                        pe.wait_ge(bank_emptied, order(i, "turn_h1") + 1)
                        project_turned(i, "k1", W["k1"], turned_in)

                def project_v1():
                    if active(i, PROJECT):
                        pe.wait_ge(bank_emptied, order(i, "turn_h1") + 1)
                        project(i, "v1", W["v1"], turned_in)

                def project_out1():
                    if active(i, SELF):
                        pe.wait_ge(bank_emptied, order(i, "turn_o1") + 1)
                        project(i, "out1", W["o1"], turned_o)

                turn_ctx()
                self_scores(0)
                turn_o2()
                turn_h2()
                self_scores(1)
                project_k2()
                project_out2()
                self_scores(2)
                project_q2()
                self_scores(3)
                self_weights(0)
                self_weights(1)
                self_scores(4)
                project_v2()
                turn_h3()
                self_weights(2)
                self_scores(5)
                turn_h1()
                self_weights(3)
                self_scores(6)
                route()
                self_scores(7)
                project_k1()
                expert_pair(0)
                project_q1()
                expert_pair(1)
                cross_scores(0)
                project_v1()
                cross_scores(1)
                self_weights(4)
                expert_pair(2)
                expert_pair(3)
                expert_pair(4)
                cross_scores(2)
                expert_pair(5)
                self_weights(5)
                cross_scores(3)
                expert_pair(6)
                expert_pair(7)
                cross_turn(0)
                self_weights(6)
                cross_scores(4)
                self_weights(7)
                cross_turn(1)
                cross_scores(5)
                cross_attend(0)
                cross_turn(2)
                cross_scores(6)
                cross_attend(1)
                cross_turn(3)
                cross_attend(2)
                cross_scores(7)
                cross_turn(4)
                turn_o1()
                cross_attend(3)
                cross_turn(5)
                cross_attend(4)
                project_out1()
                cross_turn(6)
                cross_attend(5)
                cross_turn(7)
                cross_attend(6)
                cross_attend(7)

            pipeline(pe, iteration)


_INS = ["x", "ctx_1024"] + [f"L0_{a}_{w}" for a in ("attn", "xattn")
                            for w in ("Wq", "bq", "Wk", "bk", "Wv", "bv", "Wo", "bo")] \
    + ["L0_ffn_router_w", "L0_ffn_expert_weights"]


def kernel(**inputs):
    import numpy as _np
    import concourse.bacc as _bacc
    from concourse import mybir as _mybir
    from concourse.bass_utils import run_bass_kernel_spmd as _run

    nc = _bacc.Bacc("TRN2", target_bir_lowering=False, num_devices=1)
    arrays, args = {}, []
    for name in _INS:
        a = _np.ascontiguousarray(inputs[name])
        arrays[f"in_{name}"] = a
        args.append(nc.dram_tensor(f"in_{name}", a.shape, _mybir.dt.from_np(a.dtype), kind="ExternalInput").ap())
    shape = inputs["x"].shape
    args.append(nc.dram_tensor("out_0", shape, _mybir.dt.float32, kind="ExternalOutput").ap())
    decoder_layer(nc, *args)
    r = _run(nc, [arrays], core_ids=[0])
    return r.results[0]["out_0"]
```

```python
from contextlib import ExitStack

import concourse.bass as bass
from concourse import mybir

F32 = mybir.dt.float32
F32R = mybir.dt.float32r
ACT = mybir.ActivationFunctionType
ALU = mybir.AluOpType
AX = mybir.AxisListType

P = 128
EPS = 1e-5
TOP_EPS = 1e-6
WINDOW = 128
MASKED = 1e30
PAIR = 2

PROJECT, SELF, CROSS, EXPERTS = range(4)
STAGES = 4

BANK_USERS = [
    ("turn_ctx", CROSS, True), ("turn_h2", CROSS, True), ("turn_o2", EXPERTS, True),
    ("out2", EXPERTS, False), ("k2", CROSS, True), ("q2", CROSS, True),
    ("v2", CROSS, False), ("turn_h3", EXPERTS, True), ("turn_h1", PROJECT, True),
    ("k1", PROJECT, True), ("q1", PROJECT, True), ("v1", PROJECT, False),
    ("turn_o1", SELF, True), ("out1", SELF, False),
]
BANKS = 3


def decoder_layer(nc, x, ctx, wq1, bq1, wk1, bk1, wv1, bv1, wo1, bo1,
                  wq2, bq2, wk2, bk2, wv2, bv2, wo2, bo2, router, experts, out):
    BATCHES, TOK, D = x.shape
    EX = router.shape[0]
    HEADS = 16
    HD = D // HEADS
    C = D // P
    NG = BATCHES // PAIR
    ROWS = 3 * HD
    UNITS = HEADS // 2
    FUNITS = PAIR * EX // 2
    TOK2 = PAIR * TOK
    SCALE1 = float(D) ** -0.5
    SCALE2 = float(HD) ** -0.5
    assert TOK == P and D == C * P and BATCHES % PAIR == 0 and 2 * ROWS <= P and UNITS % 4 == 0
    FIRST, LAST = STAGES, NG
    FIRST_WEIGHTS = 3

    def active(i, stage):
        return not isinstance(i, int) or 0 <= i - stage < NG

    def order(i, name, rounded=False):
        users = [(n, s) for n, s, r in BANK_USERS if r or not rounded]
        at = [n for n, _ in users].index(name)
        if isinstance(i, int):
            return (sum(active(k, s) for k in range(i) for _, s in users)
                    + sum(active(i, s) for _, s in users[:at]))
        return order(FIRST, users[0][0], rounded) + len(users) * (i - FIRST) + at

    def bank_of(name):
        return [n for n, _, _ in BANK_USERS].index(name) % BANKS

    def emptied_before(i, name):
        if not isinstance(i, int):
            return order(i, name) - BANKS + 1
        at = [n for n, _, _ in BANK_USERS].index(name)
        before = [(k, p) for k in range(i + 1) for p, (_, s, _) in enumerate(BANK_USERS)
                  if (k, p) < (i, at) and p % BANKS == at % BANKS and active(k, s)]
        return order(before[-1][0], BANK_USERS[before[-1][1]][0]) + 1 if before else 0

    def wait(eng, sem, value):
        if not isinstance(value, int) or value > 0:
            eng.wait_ge(sem, value)

    def wait_alone(eng, sem, value):
        if not isinstance(value, int) or value > 0:
            eng.wait_ge(sem, value)
            eng.sem_inc(passed[eng.engine], 1)

    stack = ExitStack()
    with stack:
        def sb(name, shape, dt=F32):
            return stack.enter_context(nc.sbuf_tensor(name, shape, dt))

        def ps(name, shape):
            return stack.enter_context(nc.psum_tensor(name, shape, F32))

        def sem(name):
            return stack.enter_context(nc.semaphore(name))

        names = ["q1", "k1", "v1", "o1", "q2", "k2", "v2", "o2"]
        w_dram = dict(zip(names, [wq1, wk1, wv1, wo1, wq2, wk2, wv2, wo2]))
        w_scale = {n: {"q1": SCALE1, "k1": SCALE1, "q2": SCALE2, "k2": -1.0}.get(n, 1.0) for n in names}
        W = {n: sb(f"w_{n}", [P, 2, C, D], F32R) for n in names}
        WE = sb("w_experts", [P, 2, C, EX * D], F32R)
        router_raw = sb("router_raw", [EX, D])
        router_t = sb("router_t", [P, 2, C, EX], F32R)
        b_dram = {"q1": bq1, "k1": bk1, "q2": bq2, "k2": bk2}
        bcol_raw = sb("bcol_raw", [P, 4, C])
        bcol = sb("bcol", [P, 4, C])
        B_AT = {n: k for k, n in enumerate(b_dram)}
        brow = sb("brow", [P, 4, D])
        R_AT = {"v1": 0, "o1": 1, "v2": 2, "o2": 3}
        ident = sb("ident", [P, P])
        mask = sb("mask", [P, P])
        minus_half = sb("minus_half", [P, PAIR])
        falling = sb("falling", [P, PAIR, EX])

        x_in = sb("x_in", [P, PAIR, D])
        c_in = sb("c_in", [P, PAIR, D])
        x_o1 = sb("x_o1", [P, PAIR, D])
        x1 = sb("x1", [P, PAIR, D])
        x1_o2 = sb("x1_o2", [P, PAIR, D])
        x2 = sb("x2", [P, PAIR, D])
        h = [sb(f"h{k + 1}", [P, PAIR, D]) for k in range(3)]
        stats = [sb(f"stats{k + 1}", [P, PAIR, 6]) for k in range(3)]
        moments = [sb(f"moments{k + 1}", [P, PAIR, 2]) for k in range(3)]
        rstd = [sb(f"rstd{k + 1}", [P, PAIR]) for k in range(3)]
        v1 = sb("v1", [P, PAIR, D])
        v2 = sb("v2", [P, PAIR, D])
        o1 = sb("o1", [P, PAIR, D])
        o2 = sb("o2", [P, PAIR, D])
        turned_o = sb("turned_o", [P, 2, C, TOK2], F32R)
        turned_in = sb("turned_in", [P, 2, C, TOK2], F32R)
        turned_h = sb("turned_h", [P, 2, C, TOK2], F32R)
        q_split = sb("q_split", [P, 2, C, TOK2], F32R)
        k_split = sb("k_split", [P, 2, C, TOK2], F32R)
        ks1_in = sb("ks1_in", [PAIR * ROWS, HEADS, TOK], F32R)
        ks1 = sb("ks1", [PAIR * ROWS, HEADS, TOK], F32R)
        qs1 = sb("qs1", [PAIR * ROWS, PAIR, HEADS, TOK], F32R)
        qs2 = sb("qs2", [PAIR * ROWS, HEADS, TOK], F32R)
        ks2 = sb("ks2", [PAIR * ROWS, PAIR, HEADS, TOK], F32R)
        nmax1 = sb("nmax1", [P, UNITS, 4])
        nmax2 = sb("nmax2", [P, UNITS, 4])
        sum1 = sb("sum1", [P, PAIR, HEADS])
        sum2 = sb("sum2", [P, PAIR, HEADS])
        rsum1 = sb("rsum1", [P, PAIR * HEADS * (PAIR * HEADS + 1)])
        rsum1_places = rsum1[:].rearrange("p (b e k) -> p b e k", b=PAIR, e=HEADS)[:, :, :, 0]
        rsum2 = sb("rsum2", [P, PAIR, HEADS])
        w_row = sb("w_row", [PAIR * HEADS, 8, HEADS])
        w_tok = sb("w_tok", [P, PAIR, HEADS])
        r_nmax = sb("r_nmax", [P, PAIR])
        r_exp = sb("r_exp", [P, PAIR, EX])
        r_sum = sb("r_sum", [P, PAIR])
        r_rsum = sb("r_rsum", [P, PAIR])
        r_p = sb("r_p", [P, PAIR, EX])
        r_rest = sb("r_rest", [P, PAIR, EX])
        r_eq = sb("r_eq", [P, PAIR, EX])
        r_key = sb("r_key", [P, PAIR, EX])
        r_first = sb("r_first", [P, PAIR])
        r_hot = [sb(f"r_hot{j}", [P, PAIR, EX]) for j in range(2)]
        r_top = sb("r_top", [P, PAIR, 2])
        r_norm = sb("r_norm", [P, PAIR])
        r_rnorm = sb("r_rnorm", [P, PAIR])
        r_w = sb("r_w", [P, PAIR, 2])
        r_pw = sb("r_pw", [P, PAIR, 2])
        r_wh = [sb(f"r_wh{j}", [P, PAIR, EX]) for j in range(2)]
        r_c = sb("r_c", [P, PAIR, EX])
        r_bias = sb("r_bias", [P, PAIR])
        space = sb("space", [P, 7168])
        w_raw = {n: space[:, 512 * k:512 * k + 512].rearrange("p (c n) -> p c n", c=C)
                 for k, n in enumerate(names[:6])}
        w_raw.update({n: a[:] for n, a in zip(names[6:], h[1:])})
        e_raw = space[:, 3072:7168].rearrange("p (c n) -> p c n", c=C)
        SLOTS = 4
        e1 = space[:, 0:2048].rearrange("p (s h b a) -> p s h b a", s=SLOTS, h=2, b=PAIR)
        e2 = space[:, 2048:4096].rearrange("p (s h b a) -> p s h b a", s=SLOTS, h=2, b=PAIR)
        e2_t = space[:, 4096:5120].rearrange("p (s h b a) -> p s h b a", s=2, h=2, b=PAIR)
        scaled = space[:, 5120:6144].rearrange("p (s n) -> p s n", s=4)
        y = space[:, 6144:6656].rearrange("p (b n) -> p b n", b=PAIR)

        scores = ps("scores", [P, 2, 512])
        bank = ps("bank", [P, BANKS, 512])
        turned_e = ps("turned_e", [P, 512])
        attended = ps("attended", [P, 512])
        small = ps("small", [P, 512])
        w_sum = small[0:PAIR * HEADS, 0:P]
        logits = attended[:, 0:PAIR * EX].rearrange("p (b e) -> p b e", b=PAIR)
        router_ps = small[:, 128:128 + C * EX].rearrange("p (c e) -> p c e", c=C)

        relay = {n: nc.dram_tensor(f"relay_{n}", [3, HD, HEADS, PAIR, TOK], F32, kind="Internal").ap()
                 for n in ("q1", "k1", "q2", "k2")}
        RELAY_BOTH = {"q": 1, "k": 0}
        RELAY_HIGH = {"q": 0, "k": 2}

        first_weights_in, later_weights_in = sem("first_weights_in"), sem("later_weights_in")
        experts_in, bcol_in, bias_in, router_in = sem("experts_in"), sem("bcol_in"), sem("bias_in"), sem("router_in")
        ident_zero, ident_ready, zeros_ready = sem("ident_zero"), sem("ident_ready"), sem("zeros_ready")
        mask_ready, falling_ready = sem("mask_ready"), sem("falling_ready")
        w_high, w_low, bcol_ready = sem("w_high"), sem("w_low"), sem("bcol_ready")
        router_turned, router_ready = sem("router_turned"), sem("router_ready")
        x_loaded, c_loaded, stored = sem("x_loaded"), sem("c_loaded"), sem("stored")
        bank_filled, bank_rounded, bank_emptied = sem("bank_filled"), sem("bank_rounded"), sem("bank_emptied")
        ln_stats = [sem(f"ln_stats{k + 1}") for k in range(3)]
        ln_moments = [sem(f"ln_moments{k + 1}") for k in range(3)]
        ln_rstd = [sem(f"ln_rstd{k + 1}") for k in range(3)]
        ln_done = [sem(f"ln_done{k + 1}") for k in range(3)]
        relay_in = {n: sem(f"relay_in_{n}") for n in relay}
        relay_out = {n: sem(f"relay_out_{n}") for n in relay}
        self_scored, self_maxed, self_exped = sem("self_scored"), sem("self_maxed"), sem("self_exped")
        self_inverted, self_weighed = sem("self_inverted"), sem("self_weighed")
        w_laid, w_spread, o1_ready = sem("w_laid"), sem("w_spread"), sem("o1_ready")
        k1_laid = sem("k1_laid")
        x_o1_ready, x1_ready, x1_o2_ready, x2_ready = sem("x_o1_ready"), sem("x1_ready"), sem("x1_o2_ready"), sem("x2_ready")
        cross_scored, cross_maxed, cross_exped = sem("cross_scored"), sem("cross_maxed"), sem("cross_exped")
        cross_turned, e2_by_act, e2_by_dve = sem("cross_turned"), sem("e2_by_act"), sem("e2_by_dve")
        cross_attended, cross_inverted, o2_ready = sem("cross_attended"), sem("cross_inverted"), sem("o2_ready")
        logits_ready, r_maxed, r_exped = sem("logits_ready"), sem("r_maxed"), sem("r_exped")
        r_step, routed = sem("r_step"), sem("routed")
        expert_ready, base_ready, first_summed, second_scaled, second_summed = (
            sem("expert_ready"), sem("base_ready"), sem("first_summed"), sem("second_scaled"), sem("second_summed"))

        passed = {e: sem(f"passed_{n}") for n, e in (("sp", nc.sync.engine), ("pool", nc.gpsimd.engine), ("dve", nc.vector.engine))}

        block = stack.enter_context(nc.Block())

        x_g = x.rearrange("(g b) t c -> g t b c", b=PAIR)
        c_g = ctx.rearrange("(g b) t c -> g t b c", b=PAIR)
        out_g = out.rearrange("(g b) t c -> g t b c", b=PAIR)

        def w_source(n):
            if n not in b_dram:
                return [w_raw[n]]
            return [w_raw[n][:, c, :].rearrange("p (l m x) -> p m x l", m=C, x=HD) for c in range(C)]

        def w_out(n, part):
            if n not in b_dram:
                return [W[n][:, part]]
            return [W[n][:, part, c, :].rearrange("p (m x l) -> p m x l", m=C, x=HD) for c in range(C)]

        def pipeline(eng, iteration):
            for i in range(FIRST):
                iteration(i)
            with eng.Fori(FIRST, LAST) as i:
                iteration(i)
            for i in range(LAST, NG + STAGES - 1):
                iteration(i)

        @block.sync
        def _(sp):
            with nc.allow_non_contiguous_dma("biases by channel, once"):
                sp.dma_start(x_in[:], x_g[0]).then_inc(x_loaded, 16)
                for n in names[:FIRST_WEIGHTS]:
                    sp.dma_start(w_raw[n], w_dram[n].rearrange("(c p) n -> p c n", p=P)).then_inc(first_weights_in, 16)
                for n, b in b_dram.items():
                    for m in range(C):
                        sp.dma_start(bcol_raw[:, B_AT[n], m:m + 1],
                                     b.rearrange("(l m x o) -> m x l o", m=C, x=HD, o=1)[m]).then_inc(bcol_in, 16)
                for n, b in (("v1", bv1), ("o1", bo1), ("v2", bv2), ("o2", bo2)):
                    sp.dma_start(brow[:, R_AT[n], :], b.partition_broadcast(P)).then_inc(bias_in, 16)
            for n in names[FIRST_WEIGHTS:]:
                sp.dma_start(w_raw[n], w_dram[n].rearrange("(c p) n -> p c n", p=P)).then_inc(later_weights_in, 16)
            sp.dma_start(router_raw[:], router).then_inc(router_in, 16)
            for c in range(C):
                sp.dma_start(e_raw[:, c, :].rearrange("p (e n) -> p e n", n=D),
                             experts[:, c * P:(c + 1) * P, :].rearrange("e p n -> p e n")).then_inc(experts_in, 16)
            sp.wait_ge(zeros_ready, 2)

            def relay_write(g, n, split, done):
                wait_alone(sp, bank_emptied, done)
                wait_alone(sp, relay_out[n], 2 * 16 * g)
                to = relay[n].rearrange("j x (l c) b t -> (x l) j c (b t)", c=C)
                both, high = RELAY_BOTH[n[0]], RELAY_HIGH[n[0]]
                sp.dma_start(to[:, both:both + 2].rearrange("p j c t -> p j (c t)"),
                             split[:].rearrange("p j c t -> p j (c t)").bitcast(F32)).then_inc(relay_in[n], 16)
                sp.dma_start(to[:, high].rearrange("p c t -> p (c t)"),
                             split[:, 0].rearrange("p c t -> p (c t)").bitcast(F32)).then_inc(relay_in[n], 16)

            def relay_read(g, n, target, scored, count=UNITS):
                wait_alone(sp, relay_in[n], 2 * 16 * (g + 1))
                wait_alone(sp, scored, count * g)
                for b in range(PAIR):
                    rows = target[b * ROWS:(b + 1) * ROWS]
                    sp.dma_start((rows[:, b] if len(target.shape) == 4 else rows).bitcast(F32),
                                 relay[n][:, :, :, b, :].rearrange("j x g t -> (j x) g t")).then_inc(relay_out[n], 16)

            def iteration(i):
                gp, gs, gc, ge = i - PROJECT, i - SELF, i - CROSS, i - EXPERTS

                def write_k2():
                    if active(i, CROSS):
                        relay_write(gc, "k2", k_split, order(i, "k2") + 1)

                def write_q2():
                    if active(i, CROSS):
                        relay_write(gc, "q2", q_split, order(i, "q2") + 1)

                def write_q1():
                    if active(i, PROJECT):
                        relay_write(gp, "q1", q_split, order(i, "q1") + 1)

                def write_k1():
                    if active(i, PROJECT):
                        relay_write(gp, "k1", k_split, order(i, "k1") + 1)

                def read_k2():
                    if active(i, CROSS):
                        relay_read(gc, "k2", ks2, cross_scored)

                def read_q2():
                    if active(i, CROSS):
                        relay_read(gc, "q2", qs2, cross_scored)

                def read_q1():
                    if active(i, PROJECT):
                        relay_read(gp, "q1", qs1, self_scored)

                def read_k1():
                    if active(i, PROJECT):
                        relay_read(gp, "k1", ks1_in, k1_laid, 1)

                def load_context():
                    if active(i, SELF):
                        if active(i, CROSS):
                            wait_alone(sp, bank_filled, order(i, "turn_ctx") + 1)
                        sp.dma_start(c_in[:], c_g[gs]).then_inc(c_loaded, 16)

                def load_x():
                    if active(i + 1, PROJECT):
                        wait_alone(sp, ln_done[0], gp + 1)
                        wait_alone(sp, x_o1_ready, gp + 1)
                        sp.dma_start(x_in[:], x_g[gp + 1]).then_inc(x_loaded, 16)

                def spread_w():
                    if active(i, SELF):
                        wait_alone(sp, w_laid, gs + 1)
                        wait_alone(sp, o1_ready, gs)
                        for b in range(PAIR):
                            sp.dma_start(w_tok[:, b, :], w_row[b * HEADS:(b + 1) * HEADS]).then_inc(w_spread, 16)

                def store():
                    if active(i, EXPERTS):
                        wait_alone(sp, first_summed, EX * (ge + 1))
                        wait_alone(sp, second_summed, EX * (ge + 1))
                        sp.dma_start(out_g[ge], y).then_inc(stored, 16)

                write_k2()
                load_context()
                write_q2()
                read_k2()
                read_q2()
                write_k1()
                spread_w()
                write_q1()
                read_k1()
                read_q1()
                store()
                load_x()

            for i in range(FIRST):
                iteration(i)
            with sp.Fori(FIRST, LAST - 1) as i:
                iteration(i)
            for i in range(LAST - 1, NG + STAGES - 1):
                iteration(i)
            sp.wait_ge(stored, 16 * NG)

        @block.gpsimd
        def _(pool):
            for m in (ident, mask):
                nc.gpsimd.memset(m[:], 0.0).then_inc(ident_zero, 1)
            pool.wait_ge(ident_zero, 2)
            nc.gpsimd.affine_select(out=ident[:], in_=ident[:], compare_op=ALU.not_equal, fill=1.0, base=0,
                                    pattern=[[-1, P]], channel_multiplier=1).then_inc(ident_ready, 1)
            nc.gpsimd.affine_select(out=mask[:], in_=mask[:], compare_op=ALU.is_ge, fill=MASKED,
                                    base=WINDOW // 2, pattern=[[-1, P]], channel_multiplier=1).then_inc(mask_ready, 1)
            pool.wait_ge(mask_ready, 1)
            nc.gpsimd.affine_select(out=mask[:], in_=mask[:], compare_op=ALU.is_ge, fill=MASKED,
                                    base=WINDOW // 2, pattern=[[1, P]], channel_multiplier=-1).then_inc(mask_ready, 1)
            for s in (qs1[:].bitcast(F32), ks2[:].bitcast(F32), rsum1[:]):
                nc.gpsimd.memset(s, 0.0).then_inc(zeros_ready, 1)
            for e in range(EX):
                nc.gpsimd.memset(falling[:, :, e:e + 1], float(EX - e)).then_inc(falling_ready, 1)
            nc.gpsimd.memset(minus_half[:], -0.5).then_inc(falling_ready, 1)
            pool.wait_ge(falling_ready, EX + 1)
            pool.wait_ge(bias_in, 4 * 16)

            def invert_deviation(k, g):
                wait_alone(pool, ln_moments[k], g + 1)
                nc.gpsimd.tensor_scalar(rstd[k][:], moments[k][:, :, 1], EPS, None, ALU.add).then_inc(ln_rstd[k], 1)
                pool.wait_ge(ln_rstd[k], 2 * g + 1)
                nc.gpsimd.tensor_tensor(rstd[k][:], rstd[k][:], minus_half[:], ALU.pow).then_inc(ln_rstd[k], 1)

            def add_bias(to, source, n):
                return nc.gpsimd.tensor_tensor(
                    to[:], source[:], brow[:, R_AT[n], :].unsqueeze(1).to_broadcast([P, PAIR, D]), ALU.add)

            def iteration(i):
                gp, gs, gc, ge = i - PROJECT, i - SELF, i - CROSS, i - EXPERTS

                def deviation3():
                    if active(i, EXPERTS):
                        invert_deviation(2, ge)

                def deviation1():
                    if active(i, PROJECT):
                        invert_deviation(0, gp)

                def deviation2():
                    if active(i, SELF):
                        invert_deviation(1, gs)

                def residual2():
                    if active(i, CROSS):
                        pool.wait_ge(x1_ready, gc + 1)
                        wait(pool, x2_ready, gc)
                        add_bias(x1_o2, x1, "o2").then_inc(x1_o2_ready, 1)

                def residual1():
                    if active(i, PROJECT):
                        pool.wait_ge(x_loaded, 16 * (gp + 1))
                        wait(pool, x1_ready, gp)
                        add_bias(x_o1, x_in, "o1").then_inc(x_o1_ready, 1)

                def sum_second():
                    if not active(i, EXPERTS):
                        return
                    for e in range(EX):
                        pool.wait_ge(second_scaled, EX * ge + e + 1)
                        if e:
                            pool.wait_ge(second_summed, EX * ge + e)
                        nc.gpsimd.tensor_tensor(y[:, 1, :], y[:, 1, :], scaled[:, e % 4, :] if e else x2[:, 1, :], ALU.add)\
                            .then_inc(second_summed, 1)

                def weigh_v():
                    if active(i, SELF):
                        pool.wait_ge(w_spread, 2 * 16 * (gs + 1))
                        if active(i - 1, SELF) and not (isinstance(i, int) and gs == 0):
                            pool.wait_ge(bank_filled, order(i - 1, "turn_o1") + 1)
                        nc.gpsimd.tensor_tensor(
                            o1[:].rearrange("p b (g x) -> p (b g) x", x=HD),
                            v1[:].rearrange("p b (g x) -> p (b g) x", x=HD),
                            w_tok[:].rearrange("p b g -> p (b g)").unsqueeze(2).to_broadcast([P, PAIR * HEADS, HD]),
                            ALU.mult).then_inc(o1_ready, 1)

                deviation3()
                deviation1()
                residual2()
                sum_second()
                weigh_v()
                deviation2()
                residual1()

            pipeline(pool, iteration)

        @block.scalar
        def _(act):
            def split_high(some):
                for n in some:
                    for to, source in zip(w_out(n, 0), w_source(n)):
                        last = nc.scalar.activation(to, source, ACT.Copy, scale=w_scale[n])
                    last.then_inc(w_high, 1)

            act.wait_ge(first_weights_in, FIRST_WEIGHTS * 16)
            split_high(names[:FIRST_WEIGHTS])

            def high(i, name, target):
                act.wait_ge(bank_filled, order(i, name) + 1)
                nc.scalar.activation(target[:, 0].rearrange("p c t -> p (c t)"), bank[:, bank_of(name), :], ACT.Copy)\
                    .then_inc(bank_rounded, 1)

            def high_biased(i, name, target):
                if isinstance(i, int) and i == PROJECT:
                    act.wait_ge(bcol_ready, 4)
                act.wait_ge(bank_filled, order(i, name) + 1)
                for c in range(C):
                    last = nc.scalar.activation(target[:, 0, c, :], bank[:, bank_of(name), c * TOK2:(c + 1) * TOK2],
                                                ACT.Identity, bias=bcol[:, B_AT[name], c:c + 1])
                last.then_inc(bank_rounded, 1)

            def exps(maxed, exped, g, u, nmax, e, total, sign):
                act.wait_ge(maxed, UNITS * g + u + 1)
                for hh in range(2):
                    for b in range(PAIR):
                        col = (hh * PAIR + b) * P
                        last = nc.scalar.activation(e[:, u % SLOTS, hh, b, :], scores[:, u % 2, col:col + P], ACT.Exp,
                                                    bias=nmax[:, u, hh * PAIR + b:hh * PAIR + b + 1], scale=sign,
                                                    accum_out=total[:, b, 2 * u + hh:2 * u + hh + 1])
                last.then_inc(exped, 1)

            def iteration(i):
                gp, gs, gc, ge = i - PROJECT, i - SELF, i - CROSS, i - EXPERTS

                def split_later():
                    if isinstance(i, int) and i == PROJECT:
                        act.wait_ge(later_weights_in, (8 - FIRST_WEIGHTS) * 16)
                        split_high(names[FIRST_WEIGHTS:])
                        act.wait_ge(experts_in, C * 16)
                        for c in range(C):
                            nc.scalar.activation(WE[:, 0, c, :], e_raw[:, c, :], ACT.Copy).then_inc(w_high, 1)

                def self_exps(u):
                    if active(i, SELF):
                        if isinstance(i, int) and i == SELF and u == 0:
                            act.wait_ge(w_low, 8)
                        wait(act, self_weighed, UNITS * gs + u + 1 - SLOTS)
                        exps(self_maxed, self_exped, gs, u, nmax1, e1, sum1, 1.0)

                def cross_exps(u):
                    if active(i, CROSS):
                        if isinstance(i, int) and i == CROSS and u == 0:
                            act.wait_ge(w_low, 8 + C)
                        wait(act, cross_turned, UNITS * gc + u + 1 - SLOTS)
                        exps(cross_maxed, cross_exped, gc, u, nmax2, e2, sum2, -1.0)

                def copy_turned(u):
                    if active(i, CROSS):
                        act.wait_ge(cross_turned, UNITS * gc + u + 1)
                        wait(act, cross_attended, UNITS * gc + u - 1)
                        nc.scalar.activation(e2_t[:, 0].rearrange("p h b a -> p (h b a)"), turned_e[:], ACT.Copy)\
                            .then_inc(e2_by_act, 1)

                def scale_second(q):
                    if not active(i, EXPERTS):
                        return
                    act.wait_ge(expert_ready, FUNITS * ge + 2 * q + 2)
                    if q == 0:
                        act.wait_ge(routed, ge + 1)
                        wait(act, stored, 16 * ge)
                    for e in (2 * q, 2 * q + 1):
                        source = attended[:, (e % 2) * D:(e % 2 + 1) * D]
                        if e == 0:
                            ins = nc.scalar.activation(y[:, 1, :], source, ACT.Identity,
                                                       bias=r_bias[:, 1:2], scale=r_c[:, 1, 0:1])
                        else:
                            wait(act, second_summed, EX * ge + (e - 3 if e > 4 else 0))
                            ins = nc.scalar.activation(scaled[:, e % 4, :], source, ACT.Copy, scale=r_c[:, 1, e:e + 1])
                        ins.then_inc(second_scaled, 1)

                def first_base():
                    if active(i, EXPERTS):
                        act.wait_ge(routed, ge + 1)
                        wait(act, stored, 16 * ge)
                        nc.scalar.activation(y[:, 0, :], x2[:, 0, :], ACT.Identity, bias=r_bias[:, 0:1])\
                            .then_inc(base_ready, 1)

                def router_exps():
                    if active(i, EXPERTS):
                        act.wait_ge(r_maxed, ge + 1)
                        for b in range(PAIR):
                            last = nc.scalar.activation(r_exp[:, b, :], logits[:, b, :], ACT.Exp, bias=r_nmax[:, b:b + 1],
                                                        accum_out=r_sum[:, b:b + 1])
                        last.then_inc(r_exped, 1)

                def high_o2():
                    if active(i, EXPERTS):
                        high(i, "turn_o2", turned_o)

                def high_ctx():
                    if active(i, CROSS):
                        high(i, "turn_ctx", turned_in)

                def high_h2():
                    if active(i, CROSS):
                        high(i, "turn_h2", turned_h)

                def high_k2():
                    if active(i, CROSS):
                        wait(act, relay_in["k1"], 2 * 16 * (min(i, NG) if isinstance(i, int) else i))
                        high_biased(i, "k2", k_split)

                def high_q2():
                    if active(i, CROSS):
                        wait(act, relay_in["q1"], 2 * 16 * (min(i, NG) if isinstance(i, int) else i))
                        high_biased(i, "q2", q_split)

                def high_h3():
                    if active(i, EXPERTS):
                        high(i, "turn_h3", turned_h)

                def high_h1():
                    if active(i, PROJECT):
                        high(i, "turn_h1", turned_in)

                def high_q1():
                    if active(i, PROJECT):
                        if active(i, CROSS):
                            act.wait_ge(relay_in["q2"], 2 * 16 * (gc + 1))
                        else:
                            wait(act, relay_in["q1"], 2 * 16 * gp)
                        high_biased(i, "q1", q_split)

                def high_k1():
                    if active(i, PROJECT):
                        if active(i, CROSS):
                            act.wait_ge(relay_in["k2"], 2 * 16 * (gc + 1))
                        else:
                            wait(act, relay_in["k1"], 2 * 16 * gp)
                        high_biased(i, "k1", k_split)

                def high_o1():
                    if active(i, SELF):
                        high(i, "turn_o1", turned_o)

                high_ctx()
                high_h2()
                high_o2()
                self_exps(0)
                high_k2()
                self_exps(1)
                self_exps(2)
                high_q2()
                self_exps(3)
                high_h3()
                self_exps(4)
                high_h1()
                self_exps(5)
                router_exps()
                self_exps(6)
                high_k1()
                self_exps(7)
                first_base()
                scale_second(0)
                high_q1()
                split_later()
                cross_exps(0)
                cross_exps(1)
                scale_second(1)
                cross_exps(2)
                scale_second(2)
                cross_exps(3)
                copy_turned(0)
                scale_second(3)
                cross_exps(4)
                copy_turned(2)
                cross_exps(5)
                copy_turned(4)
                high_o1()
                cross_exps(6)
                cross_exps(7)
                copy_turned(6)

            pipeline(act, iteration)

        @block.vector
        def _(dve):
            def split_low(some):
                for n in some:
                    dve.wait_ge(w_high, names.index(n) + 1)
                    for to, source, high_part in zip(w_out(n, 1), w_source(n), w_out(n, 0)):
                        last = nc.vector.scalar_tensor_tensor(out=to, in0=source, scalar=w_scale[n], in1=high_part,
                                                              op0=ALU.mult, op1=ALU.subtract)
                    last.then_inc(w_low, 1)

            split_low(names[:FIRST_WEIGHTS])

            def low(i, name, target):
                dve.wait_ge(bank_rounded, order(i, name, rounded=True) + 1)
                nc.vector.tensor_tensor(target[:, 1].rearrange("p c t -> p (c t)"), bank[:, bank_of(name), :],
                                        target[:, 0].rearrange("p c t -> p (c t)"), ALU.subtract)\
                    .then_inc(bank_emptied, 1)

            def low_biased(i, name, target):
                dve.wait_ge(bank_rounded, order(i, name, rounded=True) + 1)
                for c in range(C):
                    last = nc.vector.scalar_tensor_tensor(
                        out=target[:, 1, c, :], in0=bank[:, bank_of(name), c * TOK2:(c + 1) * TOK2],
                        scalar=bcol[:, B_AT[name], c:c + 1], in1=target[:, 0, c, :], op0=ALU.add, op1=ALU.subtract)
                last.then_inc(bank_emptied, 1)

            def statistics(k, g, source, ready):
                for b in range(PAIR):
                    last = nc.vector.bn_stats(stats[k][:, b, :], source[:, b, :])
                last.then_inc(ready, 1)
                wait_alone(dve, ready, g + 1)
                for b in range(PAIR):
                    last = nc.vector.bn_aggr(moments[k][:, b, :], stats[k][:, b, :])
                last.then_inc(ln_moments[k], 1)

            def normalize(k, g, source):
                dve.wait_ge(ln_rstd[k], 2 * g + 2)
                for b in range(PAIR):
                    last = nc.vector.tensor_scalar(h[k][:, b, :], source[:, b, :], moments[k][:, b, 0:1],
                                                   rstd[k][:, b:b + 1], ALU.subtract, ALU.mult)
                last.then_inc(ln_done[k], 1)

            def maxima(scored, maxed, g, u, nmax):
                dve.wait_ge(scored, UNITS * g + u + 1)
                nc.vector.tensor_reduce(nmax[:, u, :], scores[:, u % 2, :].rearrange("p (s a) -> p s a", a=P), AX.X,
                                        ALU.max, negate=True).then_inc(maxed, 1)

            def in_bank(name):
                return bank[:, bank_of(name), :].rearrange("p (b n) -> p b n", b=PAIR)

            def with_bias(i, name, to, done):
                dve.wait_ge(bank_filled, order(i, name) + 1)
                wait(dve, *done)
                nc.vector.tensor_tensor(to[:], in_bank(name),
                                        brow[:, R_AT[name], :].unsqueeze(1).to_broadcast([P, PAIR, D]), ALU.add)\
                    .then_inc(bank_emptied, 1)

            def iteration(i):
                gp, gs, gc, ge = i - PROJECT, i - SELF, i - CROSS, i - EXPERTS

                def split_later():
                    if isinstance(i, int) and i == PROJECT:
                        split_low(names[FIRST_WEIGHTS:])
                        dve.wait_ge(router_turned, 1)
                        nc.vector.tensor_copy(router_t[:, 0], router_ps).then_inc(router_ready, 1)
                        dve.wait_ge(router_ready, 1)
                        nc.vector.tensor_tensor(router_t[:, 1], router_ps, router_t[:, 0], ALU.subtract)\
                            .then_inc(router_ready, 1)
                        dve.wait_ge(falling_ready, EX)
                        dve.wait_ge(mask_ready, 2)
                        dve.wait_ge(zeros_ready, 3)
                        for c in range(C):
                            dve.wait_ge(w_high, 8 + c + 1)
                            nc.vector.tensor_tensor(WE[:, 1, c, :], e_raw[:, c, :], WE[:, 0, c, :], ALU.subtract)\
                                .then_inc(w_low, 1)

                def self_max(u):
                    if active(i, SELF):
                        maxima(self_scored, self_maxed, gs, u, nmax1)

                def self_invert(u):
                    if active(i, SELF):
                        dve.wait_ge(self_exped, UNITS * gs + u + 1)
                        nc.vector.reciprocal(rsum1_places[:, :, 2 * u:2 * u + 2], sum1[:, :, 2 * u:2 * u + 2])\
                            .then_inc(self_inverted, 1)

                def cross_max(u):
                    if active(i, CROSS):
                        wait_alone(dve, cross_scored, UNITS * gc + u + 1)
                        for s in range(4):
                            block = scores[:, u % 2, s * P:(s + 1) * P]
                            last = nc.vector.tensor_tensor_reduce(block, block, mask[:], 1.0, MASKED, ALU.add, ALU.min,
                                                                  nmax2[:, u, s:s + 1])
                        last.then_inc(cross_maxed, 1)

                def copy_turned(u):
                    if active(i, CROSS):
                        dve.wait_ge(cross_turned, UNITS * gc + u + 1)
                        wait(dve, cross_attended, UNITS * gc + u - 1)
                        nc.vector.tensor_copy(e2_t[:, 1].rearrange("p h b a -> p (h b a)"), turned_e[:])\
                            .then_inc(e2_by_dve, 1)

                def sum_first(q):
                    if not active(i, EXPERTS):
                        return
                    dve.wait_ge(expert_ready, FUNITS * ge + 2 * q + 1)
                    for e in (2 * q, 2 * q + 1):
                        if e == 0:
                            dve.wait_ge(base_ready, ge + 1)
                        else:
                            dve.wait_ge(first_summed, EX * ge + e)
                        nc.vector.scalar_tensor_tensor(
                            out=y[:, 0, :], in0=turned_e[:, (e % 2) * D:(e % 2 + 1) * D], scalar=r_c[:, 0, e:e + 1],
                            in1=y[:, 0, :], op0=ALU.mult, op1=ALU.add).then_inc(first_summed, 1)

                STEPS = 18
                done = [0]

                def step(ins):
                    done[0] += 1
                    ins.then_inc(r_step, 1)
                    dve.wait_ge(r_step, STEPS * ge + done[0])

                def wide(a, n):
                    return a.unsqueeze(2).to_broadcast([P, PAIR, n])

                def router_max():
                    if active(i, EXPERTS):
                        dve.wait_ge(logits_ready, ge + 1)
                        nc.vector.tensor_reduce(r_nmax[:], logits, AX.X, ALU.max, negate=True).then_inc(r_maxed, 1)

                def route():
                    if not active(i, EXPERTS):
                        return
                    dve.wait_ge(r_exped, ge + 1)
                    step(nc.vector.reciprocal(r_rsum[:], r_sum[:]))
                    step(nc.vector.tensor_tensor(r_p[:], r_exp[:], wide(r_rsum[:], EX), ALU.mult))
                    p = r_p
                    for j in range(2):
                        step(nc.vector.tensor_reduce(r_top[:, :, j], p[:], AX.X, ALU.max))
                        step(nc.vector.tensor_tensor(r_eq[:], p[:], wide(r_top[:, :, j], EX), ALU.is_equal))
                        step(nc.vector.tensor_tensor(r_key[:], r_eq[:], falling[:], ALU.mult))
                        step(nc.vector.tensor_reduce(r_first[:], r_key[:], AX.X, ALU.max))
                        step(nc.vector.tensor_tensor(r_hot[j][:], falling[:], wide(r_first[:], EX), ALU.is_equal))
                        if j == 0:
                            step(nc.vector.scalar_tensor_tensor(out=r_rest[:], in0=r_hot[0][:], scalar=-2.0, in1=r_p[:],
                                                                op0=ALU.mult, op1=ALU.add))
                            p = r_rest
                    step(nc.vector.scalar_tensor_tensor(out=r_norm[:], in0=r_top[:, :, 0], scalar=TOP_EPS,
                                                        in1=r_top[:, :, 1], op0=ALU.add, op1=ALU.add))
                    step(nc.vector.reciprocal(r_rnorm[:], r_norm[:]))
                    step(nc.vector.tensor_tensor(r_w[:], r_top[:], wide(r_rnorm[:], 2), ALU.mult))
                    nc.vector.tensor_tensor(r_wh[0][:], r_hot[0][:], wide(r_w[:, :, 0], EX), ALU.mult)
                    nc.vector.tensor_tensor(r_wh[1][:], r_hot[1][:], wide(r_w[:, :, 1], EX), ALU.mult)
                    step(nc.vector.tensor_tensor(r_pw[:], r_top[:], r_w[:], ALU.mult))
                    nc.vector.tensor_reduce(r_bias[:], r_pw[:], AX.X, ALU.add)
                    step(nc.vector.tensor_tensor(r_c[:], r_wh[0][:], r_wh[1][:], ALU.add))
                    assert done[0] == STEPS, done
                    nc.vector.tensor_copy(r_key[:, :, 0:1], r_c[:, :, 0:1]).then_inc(routed, 1)

                def low_o2():
                    if active(i, EXPERTS):
                        low(i, "turn_o2", turned_o)

                def low_ctx():
                    if active(i, CROSS):
                        low(i, "turn_ctx", turned_in)

                def low_h2():
                    if active(i, CROSS):
                        low(i, "turn_h2", turned_h)

                def add_x2():
                    if active(i, EXPERTS):
                        dve.wait_ge(bank_filled, order(i, "out2") + 1)
                        dve.wait_ge(x1_o2_ready, ge + 1)
                        wait(dve, second_summed, EX * ge)
                        nc.vector.tensor_tensor(x2[:], in_bank("out2"), x1_o2[:], ALU.add).then_inc(bank_emptied, 1)
                        dve.wait_ge(bank_emptied, order(i, "out2") + 1)
                        statistics(2, ge, x2, x2_ready)

                def normalize3():
                    if active(i, EXPERTS):
                        normalize(2, ge, x2)

                def low_k2():
                    if active(i, CROSS):
                        low_biased(i, "k2", k_split)

                def low_q2():
                    if active(i, CROSS):
                        low_biased(i, "q2", q_split)

                def add_v2():
                    if active(i, CROSS):
                        with_bias(i, "v2", v2, (cross_attended, UNITS * gc))

                def low_h3():
                    if active(i, EXPERTS):
                        low(i, "turn_h3", turned_h)

                def statistics1():
                    if active(i, PROJECT):
                        dve.wait_ge(x_loaded, 16 * (gp + 1))
                        statistics(0, gp, x_in, ln_stats[0])

                def normalize1():
                    if active(i, PROJECT):
                        if active(i - 1, PROJECT):
                            dve.wait_ge(bank_filled, order(i - 1, "turn_h1") + 1)
                        normalize(0, gp, x_in)
                    if isinstance(i, int) and i == PROJECT:
                        dve.wait_ge(bcol_in, 4 * C * 16)
                        for n in b_dram:
                            nc.vector.tensor_scalar(bcol[:, B_AT[n], :], bcol_raw[:, B_AT[n], :], w_scale[n], None,
                                                    ALU.mult).then_inc(bcol_ready, 1)
                        dve.wait_ge(bcol_ready, 4)

                def copy_w_row():
                    if active(i, SELF):
                        dve.wait_ge(self_weighed, UNITS * (gs + 1))
                        wait(dve, w_spread, 2 * 16 * gs)
                        nc.vector.tensor_copy(w_row[:], w_sum.rearrange("p (g t) -> p t g", t=8)).then_inc(w_laid, 1)

                def low_h1():
                    if active(i, PROJECT):
                        low(i, "turn_h1", turned_in)

                def low_q1():
                    if active(i, PROJECT):
                        low_biased(i, "q1", q_split)

                def low_k1():
                    if active(i, PROJECT):
                        low_biased(i, "k1", k_split)

                def low_o1():
                    if active(i, SELF):
                        low(i, "turn_o1", turned_o)

                def add_v1():
                    if active(i, PROJECT):
                        if isinstance(i, int) and i == PROJECT:
                            dve.wait_ge(bias_in, 4 * 16)
                        with_bias(i, "v1", v1, (o1_ready, gp))

                def add_x1():
                    if active(i, SELF):
                        dve.wait_ge(bank_filled, order(i, "out1") + 1)
                        dve.wait_ge(x_o1_ready, gs + 1)
                        wait(dve, x1_o2_ready, gs)
                        nc.vector.tensor_tensor(x1[:], in_bank("out1"), x_o1[:], ALU.add).then_inc(bank_emptied, 1)
                        dve.wait_ge(bank_emptied, order(i, "out1") + 1)
                        statistics(1, gs, x1, x1_ready)

                def normalize2():
                    if active(i, SELF):
                        if active(i, CROSS):
                            dve.wait_ge(bank_filled, order(i, "turn_h2") + 1)
                        normalize(1, gs, x1)

                def divide_o2():
                    if active(i, CROSS):
                        dve.wait_ge(cross_exped, UNITS * (gc + 1))
                        nc.vector.reciprocal(rsum2[:], sum2[:]).then_inc(cross_inverted, 1)
                        dve.wait_ge(cross_inverted, gc + 1)
                        dve.wait_ge(cross_attended, UNITS * (gc + 1))
                        if active(i, EXPERTS):
                            dve.wait_ge(bank_filled, order(i, "turn_o2") + 1)
                        nc.vector.tensor_tensor(
                            o2[:].rearrange("p b (g x) -> p (b g) x", x=HD),
                            attended[:].rearrange("p (s x) -> p s x", x=HD),
                            rsum2[:].rearrange("p b g -> p (b g)").unsqueeze(2).to_broadcast([P, PAIR * HEADS, HD]),
                            ALU.mult).then_inc(o2_ready, 1)

                def lay_k1():
                    if active(i, PROJECT):
                        dve.wait_ge(relay_out["k1"], 2 * 16 * (gp + 1))
                        wait(dve, self_scored, UNITS * gp)
                        nc.vector.tensor_copy(ks1[:].rearrange("r e (g t) -> r e g t", t=8),
                                              ks1_in[:].rearrange("r g (e t) -> r e g t", t=8)).then_inc(k1_laid, 1)

                self_max(0)
                low_ctx()
                low_h2()
                low_o2()
                self_max(1)
                statistics1()
                self_invert(0)
                add_x2()
                self_max(2)
                low_k2()
                normalize3()
                normalize1()
                self_invert(1)
                self_max(3)
                low_q2()
                self_invert(2)
                self_max(4)
                self_invert(3)
                add_v2()
                low_h3()
                self_max(5)
                self_invert(4)
                low_h1()
                self_max(6)
                self_invert(5)
                router_max()
                self_max(7)
                route()
                self_invert(6)
                low_k1()
                sum_first(0)
                cross_max(0)
                cross_max(1)
                sum_first(1)
                self_invert(7)
                cross_max(2)
                low_q1()
                sum_first(2)
                cross_max(3)
                sum_first(3)
                copy_w_row()
                cross_max(4)
                copy_turned(1)
                cross_max(5)
                copy_turned(3)
                cross_max(6)
                add_v1()
                split_later()
                cross_max(7)
                low_o1()
                copy_turned(5)
                lay_k1()
                add_x1()
                copy_turned(7)
                normalize2()
                divide_o2()

            pipeline(dve, iteration)

        @block.tensor
        def _(pe):
            pe.wait_ge(ident_ready, 1)
            pe.wait_ge(w_low, FIRST_WEIGHTS)

            PRODUCTS = ((0, 0), (0, 1), (1, 0))

            def turn(i, name, source):
                wait(pe, bank_emptied, emptied_before(i, name))
                for c in range(C):
                    for b in range(PAIR):
                        last = nc.tensor.transpose(bank[:, bank_of(name), (c * PAIR + b) * P:(c * PAIR + b + 1) * P],
                                                   source[:, b, c * P:(c + 1) * P], ident[:])
                last.then_inc(bank_filled, 1)

            def project_turned(i, name, weights, turned, m):
                if m == 0:
                    wait(pe, bank_emptied, emptied_before(i, name))
                for k, (wp, xp) in enumerate(PRODUCTS):
                    for c in range(C):
                        last = nc.tensor.matmul(
                            bank[:, bank_of(name), m * TOK2:(m + 1) * TOK2], weights[:, wp, c, m * P:(m + 1) * P],
                            turned[:, xp, c, :], start=(k == 0 and c == 0), stop=(k == 2 and c == C - 1))
                if m == C - 1:
                    last.then_inc(bank_filled, 1)

            def project(i, name, weights, turned, b):
                if b == 0:
                    wait(pe, bank_emptied, emptied_before(i, name))
                for k, (wp, xp) in enumerate(PRODUCTS):
                    for c in range(C):
                        last = nc.tensor.matmul(
                            bank[:, bank_of(name), b * D:(b + 1) * D], turned[:, xp, c, b * TOK:(b + 1) * TOK],
                            weights[:, wp, c, :], start=(k == 0 and c == 0), stop=(k == 2 and c == C - 1))
                if b == PAIR - 1:
                    last.then_inc(bank_filled, 1)

            def iteration(i):
                gp, gs, gc, ge = i - PROJECT, i - SELF, i - CROSS, i - EXPERTS

                def turn_router():
                    if isinstance(i, int) and i == PROJECT:
                        pe.wait_ge(router_in, 16)
                        for c in range(C):
                            last = nc.tensor.transpose(router_ps[:, c, :], router_raw[:, c * P:(c + 1) * P],
                                                       ident[0:EX, 0:EX])
                        last.then_inc(router_turned, 1)

                def self_scores(u):
                    if not active(i, SELF):
                        return
                    if u == 0:
                        pe.wait_ge(relay_out["q1"], 2 * 16 * (gs + 1))
                        pe.wait_ge(k1_laid, gs + 1)
                    wait(pe, self_exped, UNITS * gs + u - 1)
                    if u < 2:
                        wait(pe, cross_exped, UNITS * (gs - 1))
                    for hh in range(2):
                        e = 2 * u + hh
                        t = 8 * e
                        last = nc.tensor.matmul(scores[:, u % 2, hh * TOK2:(hh + 1) * TOK2],
                                                ks1[:, e, :], qs1[:, :, :, t:t + 8], start=True, stop=True)
                    last.then_inc(self_scored, 1)

                def self_weights(u):
                    if not active(i, SELF):
                        return
                    if isinstance(i, int) and i == SELF and u == 0:
                        pe.wait_ge(router_ready, 2)
                        pe.wait_ge(w_low, 8)
                    pe.wait_ge(self_inverted, UNITS * gs + u + 1)
                    if u == 0:
                        wait(pe, w_laid, gs)
                    for hh in range(2):
                        for b in range(PAIR):
                            e = 2 * u + hh
                            row = b * HEADS + e
                            last = nc.tensor.matmul(w_sum, rsum1[:, PAIR * HEADS * row:PAIR * HEADS * (row + 1)],
                                                    e1[:, u % SLOTS, hh, b, :], start=(u == 0 and hh == 0 and b == 0),
                                                    stop=(u == UNITS - 1 and hh == 1 and b == PAIR - 1))
                    last.then_inc(self_weighed, 1)

                def cross_scores(u):
                    if not active(i, CROSS):
                        return
                    if u == 0:
                        pe.wait_ge(relay_out["q2"], 2 * 16 * (gc + 1))
                        pe.wait_ge(relay_out["k2"], 2 * 16 * (gc + 1))
                    wait(pe, cross_exped, UNITS * gc + u - 1)
                    if u < 2:
                        wait(pe, self_exped, UNITS * (min(gc + 2, NG) if isinstance(i, int) else gc + 2))
                    for hh in range(2):
                        e = 2 * u + hh
                        last = nc.tensor.matmul(scores[:, u % 2, hh * TOK2:(hh + 1) * TOK2], qs2[:, e, :],
                                                ks2[:, :, e, :], start=True, stop=True)
                    last.then_inc(cross_scored, 1)

                def cross_turn(u):
                    if not active(i, CROSS):
                        return
                    pe.wait_ge(cross_exped, UNITS * gc + u + 1)
                    if u == 0:
                        wait(pe, first_summed, EX * gc)
                        wait(pe, e2_by_dve, UNITS // 2 * gc)
                    elif u % 2:
                        pe.wait_ge(e2_by_act, UNITS // 2 * gc + u // 2 + 1)
                    else:
                        pe.wait_ge(e2_by_dve, UNITS // 2 * gc + u // 2)
                    for hh in range(2):
                        for b in range(PAIR):
                            col = (hh * PAIR + b) * P
                            last = nc.tensor.transpose(turned_e[:, col:col + P], e2[:, u % SLOTS, hh, b, :], ident[:])
                    last.then_inc(cross_turned, 1)

                def cross_attend(u):
                    if not active(i, CROSS):
                        return
                    if u == 0:
                        pe.wait_ge(bank_emptied, order(i, "v2") + 1)
                        wait(pe, second_scaled, EX * gc)
                    pe.wait_ge(*((e2_by_dve, UNITS // 2 * gc + u // 2 + 1) if u % 2 else
                                 (e2_by_act, UNITS // 2 * gc + u // 2 + 1)))
                    for hh in range(2):
                        for b in range(PAIR):
                            e = 2 * u + hh
                            at = (b * HEADS + e) * HD
                            last = nc.tensor.matmul(attended[:, at:at + HD], e2_t[:, u % 2, hh, b, :],
                                                    v2[:, b, e * HD:(e + 1) * HD], start=True, stop=True)
                    last.then_inc(cross_attended, 1)

                def route():
                    if not active(i, EXPERTS):
                        return
                    pe.wait_ge(bank_emptied, order(i, "turn_h3") + 1)
                    wait(pe, r_exped, ge)
                    for b in range(PAIR):
                        for k, (wp, xp) in enumerate(PRODUCTS):
                            for c in range(C):
                                last = nc.tensor.matmul(logits[:, b, :], turned_h[:, xp, c, b * TOK:(b + 1) * TOK],
                                                        router_t[:, wp, c, :], start=(k == 0 and c == 0),
                                                        stop=(k == 2 and c == C - 1))
                    last.then_inc(logits_ready, 1)

                def experts_half(h):
                    if not active(i, EXPERTS):
                        return
                    f = h // 2
                    first_half = h % 2 == 0
                    if first_half and f >= PAIR:
                        pe.wait_ge((first_summed, second_scaled)[f % 2], EX * ge + 2 * (f // 2))
                    if first_half and f == 0:
                        if isinstance(i, int) and i == EXPERTS:
                            pe.wait_ge(w_low, 8 + C)
                        pe.wait_ge(e2_by_dve, UNITS // 2 * (ge + 1))
                    if first_half and f == 1:
                        pe.wait_ge(r_exped, ge + 1)
                    b, col = f % PAIR, (f // PAIR) * 2 * D
                    terms = [(wp, xp, c) for wp, xp in PRODUCTS for c in range(C)]
                    for k in range(len(terms) // 2 * (h % 2), len(terms) // 2 * (h % 2 + 1)):
                        wp, xp, c = terms[k]
                        last = nc.tensor.matmul((turned_e, attended)[f % 2][:],
                                                turned_h[:, xp, c, b * TOK:(b + 1) * TOK], WE[:, wp, c, col:col + 2 * D],
                                                start=(k == 0), stop=(k == len(terms) - 1))
                    if not first_half:
                        last.then_inc(expert_ready, 1)

                def turn_o2():
                    if active(i, EXPERTS):
                        pe.wait_ge(o2_ready, ge + 1)
                        turn(i, "turn_o2", o2)

                def turn_ctx():
                    if active(i, CROSS):
                        pe.wait_ge(c_loaded, 16 * (gc + 1))
                        turn(i, "turn_ctx", c_in)

                def turn_h2():
                    if active(i, CROSS):
                        pe.wait_ge(ln_done[1], gc + 1)
                        turn(i, "turn_h2", h[1])

                def turn_h3():
                    if active(i, EXPERTS):
                        pe.wait_ge(ln_done[2], ge + 1)
                        turn(i, "turn_h3", h[2])

                def turn_h1():
                    if active(i, PROJECT):
                        pe.wait_ge(ln_done[0], gp + 1)
                        turn(i, "turn_h1", h[0])

                def turn_o1():
                    if active(i, SELF):
                        pe.wait_ge(o1_ready, gs + 1)
                        turn(i, "turn_o1", o1)

                def project_out2(part):
                    if active(i, EXPERTS):
                        pe.wait_ge(bank_emptied, order(i, "turn_o2") + 1)
                        project(i, "out2", W["o2"], turned_o, part)

                def project_k2(part):
                    if active(i, CROSS):
                        pe.wait_ge(bank_emptied, order(i, "turn_ctx") + 1)
                        project_turned(i, "k2", W["k2"], turned_in, part)

                def project_v2(part):
                    if active(i, CROSS):
                        pe.wait_ge(bank_emptied, order(i, "turn_ctx") + 1)
                        project(i, "v2", W["v2"], turned_in, part)

                def project_q2(part):
                    if active(i, CROSS):
                        pe.wait_ge(bank_emptied, order(i, "turn_h2") + 1)
                        project_turned(i, "q2", W["q2"], turned_h, part)

                def project_q1(part):
                    if active(i, PROJECT):
                        pe.wait_ge(bank_emptied, order(i, "turn_h1") + 1)
                        project_turned(i, "q1", W["q1"], turned_in, part)

                def project_k1(part):
                    if active(i, PROJECT):
                        pe.wait_ge(bank_emptied, order(i, "turn_h1") + 1)
                        project_turned(i, "k1", W["k1"], turned_in, part)

                def project_v1(part):
                    if active(i, PROJECT):
                        pe.wait_ge(bank_emptied, order(i, "turn_h1") + 1)
                        project(i, "v1", W["v1"], turned_in, part)

                def project_out1(part):
                    if active(i, SELF):
                        pe.wait_ge(bank_emptied, order(i, "turn_o1") + 1)
                        project(i, "out1", W["o1"], turned_o, part)

                self_scores(0)
                turn_ctx()
                turn_h2()
                turn_o2()
                self_scores(1)
                project_k2(0)
                project_out2(0)
                project_out2(1)
                project_k2(1)
                self_scores(2)
                project_v2(0)
                self_weights(0)
                project_q2(0)
                project_q2(1)
                self_scores(3)
                project_v2(1)
                turn_h3()
                self_scores(4)
                self_weights(1)
                self_weights(2)
                turn_h1()
                self_scores(5)
                self_weights(3)
                self_scores(6)
                route()
                project_k1(0)
                self_scores(7)
                project_k1(1)
                self_weights(4)
                experts_half(0)
                experts_half(1)
                project_q1(0)
                project_q1(1)
                experts_half(2)
                cross_scores(0)
                cross_scores(1)
                experts_half(3)
                self_weights(5)
                experts_half(4)
                experts_half(5)
                experts_half(6)
                experts_half(7)
                cross_scores(2)
                experts_half(8)
                experts_half(9)
                self_weights(6)
                experts_half(10)
                experts_half(11)
                experts_half(12)
                cross_scores(3)
                experts_half(13)
                self_weights(7)
                experts_half(14)
                project_v1(0)
                cross_turn(0)
                experts_half(15)
                cross_scores(4)
                project_v1(1)
                turn_router()
                cross_turn(1)
                cross_attend(0)
                cross_scores(5)
                cross_turn(2)
                cross_attend(1)
                cross_turn(3)
                cross_scores(6)
                cross_attend(2)
                turn_o1()
                cross_scores(7)
                cross_turn(4)
                cross_attend(3)
                cross_turn(5)
                cross_attend(4)
                project_out1(0)
                project_out1(1)
                cross_turn(6)
                cross_attend(5)
                cross_turn(7)
                cross_attend(6)
                cross_attend(7)

            pipeline(pe, iteration)


_INS = ["x", "ctx_1024"] + [f"L0_{a}_{w}" for a in ("attn", "xattn")
                            for w in ("Wq", "bq", "Wk", "bk", "Wv", "bv", "Wo", "bo")] \
    + ["L0_ffn_router_w", "L0_ffn_expert_weights"]


def kernel(**inputs):
    import numpy as _np
    import concourse.bacc as _bacc
    from concourse import mybir as _mybir
    from concourse.bass_utils import run_bass_kernel_spmd as _run

    nc = _bacc.Bacc("TRN2", target_bir_lowering=False, num_devices=1)
    arrays, args = {}, []
    for name in _INS:
        a = _np.ascontiguousarray(inputs[name])
        arrays[f"in_{name}"] = a
        args.append(nc.dram_tensor(f"in_{name}", a.shape, _mybir.dt.from_np(a.dtype), kind="ExternalInput").ap())
    shape = inputs["x"].shape
    args.append(nc.dram_tensor("out_0", shape, _mybir.dt.float32, kind="ExternalOutput").ap())
    decoder_layer(nc, *args)
    r = _run(nc, [arrays], core_ids=[0])
    return r.results[0]["out_0"]
```
